# Optimizing a Trainium2 kernel written in Bass

```python
import numpy as np
import jax
import jax.numpy as jnp

def _softmax(x, axis=-1):
    return jax.nn.softmax(x, axis=axis)

def _gelu(x):
    return jax.nn.gelu(x, approximate=True)

def _silu(x):
    return jax.nn.silu(x)

def _sigmoid(x):
    return jax.nn.sigmoid(x)

def _layernorm(x, axis=-1, eps=1e-05):
    m = jnp.mean(x, axis=axis, keepdims=True)
    v = jnp.var(x, axis=axis, keepdims=True)
    return (x - m) / jnp.sqrt(v + eps)

def _scatter_add(tgt, idx, src, axis=0):
    return tgt.at[idx].add(src)

def _segment_sum(src, seg, n):
    return jax.ops.segment_sum(src, seg, n)
kernel_name = 'mk_xattn_ffn_d1_seqx_r2_a49de9'

def setup_inputs(seed: int=0):
    np.random.seed(seed)
    _w = jnp.asarray

    def _rec_inputs():
        import jax
        import jax.numpy as jnp
        _rk = jax.random.key(seed)
        x = -0.0002928 + 1 * jax.random.normal(jax.random.fold_in(_rk, 1), (2, 2048, 512), jnp.float32)
        _lenS = 2048 - jax.random.randint(jax.random.fold_in(_rk, 7), (2,), 0, max(1, 2048 // 4) + 1, jnp.int32)
        _lenS2 = 77 - jax.random.randint(jax.random.fold_in(_rk, 8), (2,), 0, max(1, 77 // 4) + 1, jnp.int32)
        _ctx_768P = jax.random.normal(jax.random.fold_in(_rk, 11), (2, 16, 384), jnp.float32)
        _ctx_768c = jax.random.dirichlet(jax.random.fold_in(_rk, 511), 0.3 * jnp.ones((16,), jnp.float32), (2, 77))
        _ctx_768t = jnp.einsum('bsk,bkd->bsd', _ctx_768c, _ctx_768P)
        _ctx_768t = _ctx_768t * jax.lax.rsqrt(jnp.mean(jnp.square(_ctx_768t)) + 1e-12) * 0.953939
        ctx_768 = 2.09791e-05 + 1.00001 * (_ctx_768t + 0.3 * jax.random.normal(jax.random.fold_in(_rk, 611), (2, 77, 384), jnp.float32))
        return (x, ctx_768)
    x, ctx_768 = _rec_inputs()

    def _L0_xattn_setup():
        import jax, jax.numpy as jnp
        import numpy as np
        H = 8
        D = 64
        SCALE = D ** (-0.5)
        key = jax.random.key(seed)
        ks = jax.random.split(key, 7)
        B, Nq, Nkv = (2, 1024, 1024)
        Cq, Ck, I = (512, 384, H * D)
        return {'x': jax.random.normal(ks[0], (B, Nq, Cq), jnp.float32), 'context': jax.random.normal(ks[1], (B, Nkv, Ck), jnp.float32), 'Wq': jax.random.normal(ks[2], (Cq, I), jnp.float32) * Cq ** (-0.5), 'Wk': jax.random.normal(ks[3], (Ck, I), jnp.float32) * Ck ** (-0.5), 'Wv': jax.random.normal(ks[4], (Ck, I), jnp.float32) * Ck ** (-0.5), 'Wo': jax.random.normal(ks[5], (I, Cq), jnp.float32) * I ** (-0.5), 'bo': jnp.zeros((Cq,), jnp.float32)}
    _L0_xattn_all = _L0_xattn_setup()
    _L0_xattn_in = {k: v for k, v in _L0_xattn_all.items() if k in ('Wq', 'Wk', 'Wv', 'Wo', 'bo')}
    del _L0_xattn_all

    def _L0_ffn_setup():
        import jax, jax.numpy as jnp
        import numpy as np
        NUM_EXPERTS = 8
        EXPERT_CAPACITY = 2.0
        DIM = 512
        HIDDEN_DIM = 2048
        key = jax.random.key(seed)
        k_x, k_g, k_w1, k_w2 = jax.random.split(key, 4)
        n, t, d, f, e = (8, 512, DIM, HIDDEN_DIM, NUM_EXPERTS)
        x = jax.random.normal(k_x, (n, t, d), dtype=jnp.float32)
        gate_w = jax.random.normal(k_g, (e, d), dtype=jnp.float32) * 0.02
        w1 = jax.random.normal(k_w1, (e, d, f), dtype=jnp.float32) * 0.02
        w2 = jax.random.normal(k_w2, (e, f, d), dtype=jnp.float32) * 0.02
        return {'x': x, 'gate_w': gate_w, 'w1': w1, 'w2': w2}
    _L0_ffn_all = _L0_ffn_setup()
    _L0_ffn_in = {k: v for k, v in _L0_ffn_all.items() if k in ('gate_w', 'w1', 'w2')}
    del _L0_ffn_all
    return {'x': x, 'ctx_768': ctx_768, 'L0_xattn_Wq': _L0_xattn_in['Wq'], 'L0_xattn_Wk': _L0_xattn_in['Wk'], 'L0_xattn_Wv': _L0_xattn_in['Wv'], 'L0_xattn_Wo': _L0_xattn_in['Wo'], 'L0_xattn_bo': _L0_xattn_in['bo'], 'L0_ffn_gate_w': _L0_ffn_in['gate_w'], 'L0_ffn_w1': _L0_ffn_in['w1'], 'L0_ffn_w2': _L0_ffn_in['w2']}

def reference(x, ctx_768, L0_xattn_Wq, L0_xattn_Wk, L0_xattn_Wv, L0_xattn_Wo, L0_xattn_bo, L0_ffn_gate_w, L0_ffn_w1, L0_ffn_w2):
    import jax
    import jax.numpy as jnp

    def _L0_xattn_ref(x, context, Wq, Wk, Wv, Wo, bo):
        import jax, jax.numpy as jnp
        import numpy as np
        H = 8
        D = 64
        SCALE = D ** (-0.5)
        B, Nq, _ = x.shape
        Nkv = context.shape[1]
        q = (x @ Wq).reshape(B, Nq, H, D)
        k = (context @ Wk).reshape(B, Nkv, H, D)
        v = (context @ Wv).reshape(B, Nkv, H, D)
        sim = jnp.einsum('bihd,bjhd->bhij', q, k) * SCALE
        attn = jax.nn.softmax(sim, axis=-1)
        out = jnp.einsum('bhij,bjhd->bihd', attn, v).reshape(B, Nq, H * D)
        return out @ Wo + bo

    def _L0_ffn_ref(x, gate_w, w1, w2):
        import jax, jax.numpy as jnp
        import numpy as np
        NUM_EXPERTS = 8
        EXPERT_CAPACITY = 2.0
        DIM = 512
        HIDDEN_DIM = 2048
        n, t, d = x.shape
        e = gate_w.shape[0]
        k = int(EXPERT_CAPACITY * t / e)
        scores = jnp.einsum('ntd,ed->nte', x, gate_w)
        probs = jax.nn.softmax(scores, axis=-1)
        g, m = jax.lax.top_k(probs.transpose(0, 2, 1), k)
        batch_idx = jnp.arange(n)[:, None, None]
        xin = x[batch_idx, m]
        h = jnp.einsum('nekd,edf->nekf', xin, w1)
        h = jax.nn.gelu(h, approximate=False)
        h = jnp.einsum('nekf,efd->nekd', h, w2)
        out_tok = g[..., None] * h
        out = jnp.zeros((n, t, d), dtype=x.dtype).at[batch_idx, m].add(out_tok)
        return out
    x = x + _L0_xattn_ref(_layernorm(x, axis=-1), ctx_768, L0_xattn_Wq, L0_xattn_Wk, L0_xattn_Wv, L0_xattn_Wo, L0_xattn_bo)
    x = x + _L0_ffn_ref(_layernorm(x, axis=-1), L0_ffn_gate_w, L0_ffn_w1, L0_ffn_w2)
    return x

_drawn_inputs = setup_inputs


def setup_inputs(seed=0):
    import zlib

    import numpy as np

    out = dict(_drawn_inputs(seed))
    spreads = {'L0_xattn_bo': (0.0, 0.1)}
    factors = {}
    for name, (base, spread) in spreads.items():
        noise = np.random.default_rng([zlib.crc32(name.encode()), seed]).standard_normal(out[name].shape)
        drawn = base * np.exp(spread * noise) if base else spread * noise
        out[name] = jnp.asarray(drawn.astype(out[name].dtype))
    for name, factor in factors.items():
        out[name] = (out[name] * factor).astype(out[name].dtype)
    return out
```

```python
import concourse.bass as bass
from concourse import mybir
from concourse.alu_op_type import AluOpType as ALU
from contextlib import ExitStack

F32 = mybir.dt.float32
F32R = mybir.dt.float32r
BF16 = mybir.dt.bfloat16
U32 = mybir.dt.uint32
ACT = mybir.ActivationFunctionType
AX = mybir.AxisListType

P = 128
B, S, D = 2, 2048, 512
H, HD = 8, 64
J, CK = 77, 384
E, F = 8, 2048
CAP = 2 * S // E
KD, KC, KF = D // P, CK // P, F // P
HJ = H * J
HALF = HJ // 2
MAIN, REST = 6 * J, 2 * J
PAIR = 2 * J
CH = [(c * P, min(P, HJ - c * P)) for c in range(-(-HJ // P))]
NCH = len(CH)
WC = NCH * P
TPB = 2
NT = S // P
NBLK = B * NT // TPB
COLS = B * E
CT = CAP // P
EPS = 1e-5
NV = 5


def xattn_expert_choice(nc, x, ctx, wq, wk, wv, wo, bo, gate_w, w1, w2, out):
    xn2_rows = nc.dram_tensor("xn2_rows", (B * S, D), F32, kind="Internal").ap()
    x_blk = x.rearrange("b (n t p) d -> (b n) p t d", t=TPB, p=P)
    out_blk = out.rearrange("b (n t p) d -> (b n) p t d", t=TPB, p=P)
    out_rows = out.rearrange("b s d -> (b s) d")
    xn2_blk = xn2_rows.rearrange("(n t p) d -> n p t d", t=TPB, p=P)

    top = ExitStack()
    with top:
        def sb(scope, name, shape, dt=F32):
            return scope.enter_context(nc.sbuf_tensor(name, shape, dt))

        def sem(name):
            return top.enter_context(nc.semaphore(name))

        ident = sb(top, "ident", [P, P])
        ones_bf = sb(top, "ones_bf", [P, P], BF16)
        before_bf = sb(top, "before_bf", [P, P], BF16)
        col_iota = sb(top, "col_iota", [P, P], BF16)
        quarter_iota = sb(top, "quarter_iota", [P, CT], BF16)
        part_iota = sb(top, "part_iota", [P, 1], BF16)
        tile_iota = sb(top, "tile_iota", [P, B, E, NT], BF16)
        eps_c = sb(top, "eps_c", [P, TPB])
        pow_c = sb(top, "pow_c", [P, TPB])
        bo_rows = sb(top, "bo_rows", [P, TPB, D])
        gwT = sb(top, "gwT", [P, KD, E])
        probs = sb(top, "probs", [P, B, E, NT])
        tok_idx = sb(top, "tok_idx", [P, COLS, CT], U32)
        tok_gate = sb(top, "tok_gate", [P, COLS, CT])
        ps = top.enter_context(nc.psum_tensor("ps", [P, 8, 512], F32))

        attn = ExitStack()
        AH = sb(attn, "AH", [P, B, KD, HJ], F32R)
        AL = sb(attn, "AL", [P, B, KD, HJ], F32R)
        BH = sb(attn, "BH", [P, B, NCH, D], F32R)
        BL = sb(attn, "BL", [P, B, NCH, D], F32R)
        init = ExitStack()
        ctx_sb = sb(init, "ctx_sb", [J, B, CK])
        gw_sb = sb(init, "gw_sb", [E, D])
        wq_sb = sb(init, "wq_sb", [P, KD, D])
        wk_sb = sb(init, "wk_sb", [P, KC, D])
        wv_sb = sb(init, "wv_sb", [P, KC, D])
        wo_sb = sb(init, "wo_sb", [P, KD, D])
        ctxT = sb(init, "ctxT", [P, KC, B, J])
        wqT = sb(init, "wqT", [P, KD, D])
        kx = sb(init, "kx", [P, B, KD, PAIR])
        vx = sb(init, "vx", [P, B, KD, WC])
        before_f = sb(init, "before_f", [P, P])

        c_ident = sem("c_ident")
        c_zero = sem("c_zero")
        c_const = sem("c_const")
        d_ctx, d_gw, d_wk, d_wv, d_wq, d_wo, d_bo = (sem(f"d_{n}") for n in "ctx gw wk wv wq wo bo".split())
        p_ctxT = sem("p_ctxT")
        e_ctxT = sem("e_ctxT")
        p_kv = sem("p_kv")
        e_kv = sem("e_kv")
        p_wqT = sem("p_wqT")
        e_wqT = sem("e_wqT")
        p_fold = sem("p_fold")
        e_hi = sem("e_hi")
        e_lo = sem("e_lo")

        folds = [("A", b, dk) for b in range(B) for dk in range(KD)] + [("B", b, c) for b in range(B) for c in range(NCH)]

        def fold_bufs(n):
            kind, b, c = folds[n]
            pair = ps[:, 2 * (n % 4):2 * (n % 4) + 2, :]
            if kind == "A":
                src = pair[:, :, 0:HALF]
                hi, lo = (t[:, b, c, :].rearrange("p (h j) -> p h j", h=2) for t in (AH, AL))
            else:
                src = pair[:, 0, :]
                hi, lo = BH[:, b, c, :], BL[:, b, c, :]
            return src, hi, lo

        with nc.Block() as block:
            @block.sync
            def _(sp):
                sp.dma_start(ctx_sb[:], ctx.rearrange("b j c -> j b c")).then_inc(d_ctx, 16)
                sp.dma_start(gw_sb[:], gate_w).then_inc(d_gw, 16)
                sp.dma_start(wk_sb[:], wk.rearrange("(c p) n -> p c n", p=P)).then_inc(d_wk, 16)
                sp.dma_start(wv_sb[:], wv.rearrange("(c p) n -> p c n", p=P)).then_inc(d_wv, 16)
                sp.dma_start(wq_sb[:], wq.rearrange("(c p) n -> p c n", p=P)).then_inc(d_wq, 16)
                sp.dma_start(wo_sb[:], wo.rearrange("(c p) n -> p c n", p=P)).then_inc(d_wo, 16)
                for t in range(TPB):
                    sp.dma_start(bo_rows[:, t, :], bo.partition_broadcast(P)).then_inc(d_bo, 16)
                sp.wait_ge(d_bo, 16 * TPB)

            @block.gpsimd
            def _(pool):
                pool.memset(ident[:], 0.0).then_inc(c_zero, 1)
                pool.wait_ge(c_zero, 1)
                pool.affine_select(out=ident[:], in_=ident[:], compare_op=ALU.not_equal, fill=1.0, base=0,
                                   pattern=[[-1, P]], channel_multiplier=1).then_inc(c_ident, 1)
                pool.memset(before_f[:], 1.0).then_inc(c_zero, 1)
                pool.wait_ge(c_zero, 2)
                pool.affine_select(out=before_bf[:], in_=before_f[:], compare_op=ALU.is_gt, fill=0.0, base=0,
                                   pattern=[[1, P]], channel_multiplier=-1).then_inc(c_const, 1)
                pool.memset(ones_bf[:], 1.0).then_inc(c_const, 1)
                pool.memset(eps_c[:], EPS).then_inc(c_const, 1)
                pool.memset(pow_c[:], -0.5).then_inc(c_const, 1)
                pool.iota(col_iota[:], pattern=[[1, P]], base=0, channel_multiplier=0,
                          allow_small_or_imprecise_dtypes=True).then_inc(c_const, 1)
                pool.iota(quarter_iota[:], pattern=[[1, CT]], base=0, channel_multiplier=0,
                          allow_small_or_imprecise_dtypes=True).then_inc(c_const, 1)
                pool.iota(part_iota[:], pattern=[[0, 1]], base=0, channel_multiplier=1,
                          allow_small_or_imprecise_dtypes=True).then_inc(c_const, 1)
                pool.iota(tile_iota[:], pattern=[[NT, B], [0, E], [1, NT]], base=0, channel_multiplier=0,
                          allow_small_or_imprecise_dtypes=True).then_inc(c_const, 1)

            @block.tensor
            def _(pe):
                pe.wait_ge(c_ident, 1)
                pe.wait_ge(d_ctx, 16)
                for b in range(B):
                    for c in range(KC):
                        nc.tensor.transpose(ps[:, 0, (c * B + b) * J:(c * B + b + 1) * J],
                                            ctx_sb[:, b, c * P:(c + 1) * P], ident[0:J, 0:J])
                pe.wait_ge(d_gw, 16)
                for c in range(KD):
                    last = nc.tensor.transpose(ps[:, 1, c * E:(c + 1) * E], gw_sb[:, c * P:(c + 1) * P],
                                               ident[0:E, 0:E])
                last.then_inc(p_ctxT, 1)
                pe.wait_ge(e_ctxT, 1)
                for w, arrived, bank in ((wk_sb, d_wk, 2), (wv_sb, d_wv, 4)):
                    pe.wait_ge(arrived, 16)
                    for t in range(KD):
                        for c in range(KC):
                            last = nc.tensor.matmul(ps[:, bank + t // 2, (t % 2) * B * J:(t % 2 + 1) * B * J],
                                                    w[:, c, t * P:(t + 1) * P],
                                                    ctxT[:, c, :, :].rearrange("p b j -> p (b j)"),
                                                    start=(c == 0), stop=(c == KC - 1))
                    last.then_inc(p_kv, 1)
                pe.wait_ge(d_wq, 16)
                for t in range(KD):
                    bank = (0, 1, 6, 7)[t]
                    for dk in range(KD):
                        last = nc.tensor.transpose(ps[:, bank, dk * P:(dk + 1) * P],
                                                   wq_sb[:, dk, t * P:(t + 1) * P], ident[:])
                last.then_inc(p_wqT, 1)
                pe.wait_ge(e_wqT, 1)
                pe.wait_ge(e_kv, 2)
                pe.wait_ge(d_wo, 16)
                for n, (kind, b, c) in enumerate(folds):
                    if n >= 4:
                        pe.wait_ge(e_lo, n - 3)
                    if kind == "A":
                        for t in range(KD):
                            last = nc.tensor.matmul(ps[:, 2 * (n % 4) + t // 2, (t % 2) * PAIR:(t % 2 + 1) * PAIR],
                                                    wqT[:, t, c * P:(c + 1) * P], kx[:, b, t, :],
                                                    start=True, stop=True)
                    else:
                        lo, hi = c * P, (c + 1) * P
                        ts = [t for t in range(KD) if t * PAIR < hi and (t + 1) * PAIR > lo]
                        for t in ts:
                            last = nc.tensor.matmul(ps[:, 2 * (n % 4), :], vx[:, b, t, lo:hi], wo_sb[:, t, :],
                                                    start=(t == ts[0]), stop=(t == ts[-1]))
                    last.then_inc(p_fold, 1)

            @block.scalar
            def _(act):
                for n in range(len(folds)):
                    act.wait_ge(p_fold, n + 1)
                    src, hi, _ = fold_bufs(n)
                    nc.scalar.activation(hi, src, ACT.Copy).then_inc(e_hi, 1)

            @block.vector
            def _(dve):
                nc.vector.memset(kx[:], 0.0)
                nc.vector.memset(vx[:], 0.0)
                dve.wait_ge(p_ctxT, 1)
                nc.vector.tensor_copy(gwT[:].rearrange("p c e -> p (c e)"), ps[:, 1, 0:KD * E])
                nc.vector.tensor_copy(ctxT[:].rearrange("p c b j -> p (c b j)"),
                                      ps[:, 0, 0:KC * B * J]).then_inc(e_ctxT, 1)
                dve.wait_ge(e_ctxT, 1)
                for m, (dst, step, bank) in enumerate(((kx, 0, 2), (vx, PAIR, 4))):
                    dve.wait_ge(p_kv, m + 1)
                    for t in range(KD):
                        for h in range(2):
                            at = step * t + h * J
                            last = nc.vector.tensor_copy(
                                dst[h * HD:(h + 1) * HD, :, t, at:at + J],
                                ps[h * HD:(h + 1) * HD, bank + t // 2,
                                   (t % 2) * B * J:(t % 2 + 1) * B * J].rearrange("p (b j) -> p b j", b=B))
                    last.then_inc(e_kv, 1)
                dve.wait_ge(p_wqT, 1)
                for t in range(KD):
                    last = nc.vector.tensor_copy(wqT[:, t, :], ps[:, (0, 1, 6, 7)[t], :])
                last.then_inc(e_wqT, 1)
                for n in range(len(folds)):
                    dve.wait_ge(e_hi, n + 1)
                    src, hi, lo = fold_bufs(n)
                    nc.vector.tensor_tensor(lo, src, hi.bitcast(F32), ALU.subtract).then_inc(e_lo, 1)
        init.close()

        tiles = ExitStack()
        XB = sb(tiles, "XB", [P, 2, TPB, D])
        XR = sb(tiles, "XR", [P, 2, TPB, D])
        XN = sb(tiles, "XN", [P, TPB, D])
        xTh = sb(tiles, "xTh", [P, TPB, D], F32R)
        xTl = sb(tiles, "xTl", [P, TPB, D], F32R)
        PR = sb(tiles, "PR", [P, TPB, H, J])
        pTh = sb(tiles, "pTh", [P, TPB, NCH, P], F32R)
        pTl = sb(tiles, "pTl", [P, TPB, NCH, P], F32R)
        X1 = sb(tiles, "X1", [P, 2, TPB, D])
        XN2 = sb(tiles, "XN2", [P, 2, TPB, D])
        xn2T = sb(tiles, "xn2T", [P, TPB, D])
        st1 = sb(tiles, "st1", [P, TPB, 6])
        mv1 = sb(tiles, "mv1", [P, TPB, 2])
        rs1 = sb(tiles, "rs1", [P, TPB])
        ve1 = sb(tiles, "ve1", [P, TPB])
        st2 = sb(tiles, "st2", [P, TPB, 6])
        mv2 = sb(tiles, "mv2", [P, TPB, 2])
        rs2 = sb(tiles, "rs2", [P, TPB])
        ve2 = sb(tiles, "ve2", [P, TPB])
        smax = sb(tiles, "smax", [P, TPB, H])
        ssum = sb(tiles, "ssum", [P, TPB * H])
        srec = sb(tiles, "srec", [P, TPB * H])
        gmax = sb(tiles, "gmax", [P, TPB])
        gexp = sb(tiles, "gexp", [P, TPB, E])
        gsub = sb(tiles, "gsub", [P, TPB, E])
        gsum = sb(tiles, "gsum", [P, TPB])
        grec = sb(tiles, "grec", [P, TPB])

        d_x = [sem(f"d_x{i}") for i in range(2)]
        d_xr = [sem(f"d_xr{i}") for i in range(2)]
        d_x1 = [sem(f"d_x1{i}") for i in range(2)]
        d_xn2 = [sem(f"d_xn2{i}") for i in range(2)]
        (v_st1, v_mv1, g_ve1, g_rs1, v_xn, p_xT, a_xTh, v_xTl, p_s, v_max, v_sub, a_exp, v_sum, v_rec, g_prob,
         p_pT, a_pTh, v_pTl, p_o, g_xr, v_x1, v_st2, v_mv2, g_ve2, g_rs2, v_xn2, p_xn2T, a_xn2T, p_g,
         v_gmax, v_gsub, a_gexp, v_gsum, v_grec, v_gate) = (sem(n) for n in (
             "v_st1 v_mv1 g_ve1 g_rs1 v_xn p_xT a_xTh v_xTl p_s v_max v_sub a_exp v_sum v_rec g_prob "
             "p_pT a_pTh v_pTl p_o g_xr v_x1 v_st2 v_mv2 g_ve2 g_rs2 v_xn2 p_xn2T a_xn2T p_g "
             "v_gmax v_gsub a_gexp v_gsum v_grec v_gate").split())

        FIRST, LAST = -2, NBLK + 2
        LOOP = (4, NBLK - 2)

        def steps(eng, body):
            for i in range(FIRST, LOOP[0]):
                body(i, i % 2, i // 2, lambda n: 0 <= n < NBLK)
            with eng.Fori(LOOP[0] // 2, LOOP[1] // 2, 1) as k:
                for u in range(2):
                    body(2 * k + u, u, k, lambda n: True)
            for i in range(LOOP[1], LAST + 1):
                body(i, i % 2, i // 2, lambda n: 0 <= n < NBLK)

        def scores(t, part):
            return (ps[:, 2 * t, 0:MAIN], ps[:, 1, t * REST:(t + 1) * REST])[part]

        SCORES = (ps[:, 0:4:2, 0:MAIN].rearrange("p t (h j) -> p t h j", j=J),
                  ps[:, 1, 0:TPB * REST].rearrange("p (t h j) -> p t h j", t=TPB, j=J))
        HEADS = ((0, MAIN // J), (MAIN // J, H))
        TAIL = CH[-1][1]
        tails = ps[0:TAIL, 3, 0:TPB * P].rearrange("p (t q) -> p t q", q=P)
        gate_sc = ps[:, 3, 0:TPB * E].rearrange("p (t e) -> p t e", e=E)

        with nc.Block() as block:
            @block.sync
            def _(sp):
                def step(i, u, half, has):
                    lanes = []
                    if has_(has, i + 4):
                        lanes.append(("x", i + 4))
                    if has_(has, i - 2):
                        lanes.append(("out", i - 2))
                    if has_(has, i + 1):
                        lanes.append(("xr", i + 1))
                    for kind, n in lanes:
                        if kind == "x":
                            src = x_blk[n]
                            free = sp.snap(n - 1)
                            if early(i, n, 2):
                                sp.wait_ge(v_xn, free)
                            sp.dma_start(XB[:, u], src).then_inc(d_x[u], 16)
                        elif kind == "xr":
                            src = x_blk[n]
                            free = sp.snap(n - 1)
                            if early(i, n, 2):
                                sp.wait_ge(v_x1, free)
                            sp.dma_start(XR[:, 1 - u], src).then_inc(d_xr[1 - u], 16)
                        else:
                            to1, to2, done = out_blk[n], xn2_blk[n], sp.snap(n + 1)
                            sp.wait_ge(v_x1, done)
                            sp.dma_start(to1, X1[:, u]).then_inc(d_x1[u], 16)
                            sp.wait_ge(v_xn2, done)
                            sp.dma_start(to2, XN2[:, u]).then_inc(d_xn2[u], 16)

                def has_(has, n):
                    return has(n) if isinstance(n, int) else True

                def early(i, n, k):
                    return n >= k if isinstance(n, int) else True

                for n in range(2):
                    sp.dma_start(XB[:, n], x_blk[n]).then_inc(d_x[n], 16)
                for i in range(FIRST, 4):
                    step(i, i % 2, i // 2, lambda n: 0 <= n < NBLK)
                with sp.Fori(2, NBLK // 2 - 2, 1) as k:
                    for u in range(2):
                        step(2 * k + u, u, k, lambda n: True)
                for i in range(NBLK - 4, LAST + 1):
                    step(i, i % 2, i // 2, lambda n: 0 <= n < NBLK)
                for u in range(2):
                    sp.wait_ge(d_x1[u], 16 * NBLK // 2)
                    sp.wait_ge(d_xn2[u], 16 * NBLK // 2)

            @block.gpsimd
            def _(pool):
                def rstd(mv, ve, rs, ready, mid, done, n):
                    pool.wait_ge(ready, n + 1)
                    pool.tensor_tensor(ve[:], mv[:, :, 1], eps_c[:], ALU.add).then_inc(mid, 1)
                    pool.wait_ge(mid, n + 1)
                    pool.tensor_tensor(rs[:], ve[:], pow_c[:], ALU.pow).then_inc(done, 1)

                def step(i, u, half, has):
                    if has(i - 1):
                        pool.wait_ge(d_xr[1 - u], 16 * half + 16 * u)
                        pool.tensor_tensor(XR[:, 1 - u], XR[:, 1 - u], bo_rows[:], ALU.add).then_inc(g_xr, 1)
                    if has(i - 2):
                        rstd(mv2, ve2, rs2, v_mv2, g_ve2, g_rs2, i - 2)
                    if has(i + 2):
                        rstd(mv1, ve1, rs1, v_mv1, g_ve1, g_rs1, i + 2)
                    if has(i):
                        pool.wait_ge(v_rec, i + 1)
                        p = PR[:].rearrange("p t h j -> p (t h) j")
                        pool.tensor_tensor(p, p, srec[:].unsqueeze(2).broadcast_to([P, TPB * H, J]),
                                           ALU.mult).then_inc(g_prob, 1)
                steps(pool, step)

            @block.scalar
            def _(act):
                def step(i, u, half, has):
                    if has(i - 1):
                        act.wait_ge(p_pT, i)
                        nc.scalar.activation(pTh[:, :, 0:NCH - 1, :],
                                             ps[:, 6:8, :].rearrange("p t (c q) -> p t c q", q=P), ACT.Copy)
                        nc.scalar.activation(pTh[0:TAIL, :, NCH - 1, :], tails, ACT.Copy).then_inc(a_pTh, 1)
                    if has(i + 1):
                        act.wait_ge(p_xT, i + 2)
                        nc.scalar.activation(xTh[:], ps[:, 6:8, :], ACT.Copy).then_inc(a_xTh, 1)
                    if has(i):
                        act.wait_ge(v_sub, i + 1)
                        nc.scalar.activation(PR[:], PR[:], ACT.Exp, scale=HD ** -0.5).then_inc(a_exp, 1)
                    if has(i - 3):
                        act.wait_ge(v_gsub, i - 2)
                        nc.scalar.activation(gexp[:], gsub[:], ACT.Exp).then_inc(a_gexp, 1)
                    if has(i - 2):
                        act.wait_ge(p_xn2T, i - 1)
                        nc.scalar.activation(xn2T[:], ps[:, 6:8, :], ACT.Copy).then_inc(a_xn2T, 1)
                steps(act, step)

            @block.vector
            def _(dve):
                def stats(src, st, done):
                    for t in range(TPB):
                        last = nc.vector.bn_stats(st[:, t, :], src[:, t, :])
                    last.then_inc(done, 1)

                def aggregate(st, mv, done):
                    for t in range(TPB):
                        last = nc.vector.bn_aggr(mv[:, t, :], st[:, t, :])
                    last.then_inc(done, 1)

                def normalise(src, mv, rs, dst, done):
                    for t in range(TPB):
                        last = nc.vector.tensor_scalar(dst[:, t, :], src[:, t, :], mv[:, t, 0:1], rs[:, t:t + 1],
                                                       ALU.subtract, ALU.mult)
                    last.then_inc(done, 1)

                def step(i, u, half, has):
                    if has(i - 1):
                        dve.wait_ge(a_pTh, i)
                        nc.vector.tensor_tensor(pTl[:, :, 0:NCH - 1, :],
                                                ps[:, 6:8, :].rearrange("p t (c q) -> p t c q", q=P),
                                                pTh[:, :, 0:NCH - 1, :].bitcast(F32), ALU.subtract)
                        nc.vector.tensor_tensor(pTl[0:TAIL, :, NCH - 1, :], tails,
                                                pTh[0:TAIL, :, NCH - 1, :].bitcast(F32),
                                                ALU.subtract).then_inc(v_pTl, 1)
                    if has(i - 2):
                        dve.wait_ge(p_o, i - 1)
                        dve.wait_ge(g_xr, i - 1)
                        if not isinstance(i, int) or i >= 4:
                            dve.wait_ge(d_x1[u], 16 * half - 16)
                            dve.wait_ge(d_xn2[u], 16 * half - 16)
                        nc.vector.tensor_tensor(X1[:, u], ps[:, 4:6, :], XR[:, u], ALU.add).then_inc(v_x1, 1)
                        dve.wait_ge(v_x1, i - 1)
                        stats(X1[:, u], st2, v_st2)
                    if has(i + 2):
                        dve.wait_ge(d_x[u], 16 * half + 32)
                        if has(i - 2):
                            dve.wait_ge(v_st2, i - 1)
                        stats(XB[:, u], st1, v_st1)
                    elif has(i - 2):
                        dve.wait_ge(v_st2, i - 1)
                    if has(i - 2):
                        aggregate(st2, mv2, v_mv2)
                    if has(i + 2):
                        dve.wait_ge(v_st1, i + 3)
                    if has(i - 2):
                        dve.wait_ge(g_rs2, i - 1)
                        normalise(X1[:, u], mv2, rs2, XN2[:, u], v_xn2)
                    if has(i + 2):
                        aggregate(st1, mv1, v_mv1)
                    if has(i):
                        dve.wait_ge(p_s, i + 1)
                        for sc, (h0, h1) in zip(SCORES, HEADS):
                            last = nc.vector.tensor_reduce(smax[:, :, h0:h1], sc, AX.X, ALU.max)
                        last.then_inc(v_max, 1)
                        dve.wait_ge(v_max, i + 1)
                        for sc, (h0, h1) in zip(SCORES, HEADS):
                            top_of = smax[:, :, h0:h1].unsqueeze(3).broadcast_to([P, TPB, h1 - h0, J])
                            last = nc.vector.tensor_tensor(PR[:, :, h0:h1, :], sc, top_of, ALU.subtract)
                        last.then_inc(v_sub, 1)
                    if has(i - 3):
                        n = i - 3
                        dve.wait_ge(p_g, n + 1)
                        nc.vector.tensor_reduce(gmax[:], gate_sc, AX.X, ALU.max).then_inc(v_gmax, 1)
                        dve.wait_ge(v_gmax, n + 1)
                        nc.vector.tensor_tensor(gsub[:], gate_sc, gmax[:].unsqueeze(2).broadcast_to([P, TPB, E]),
                                                ALU.subtract).then_inc(v_gsub, 1)
                    if has(i + 1):
                        dve.wait_ge(a_xTh, i + 2)
                        nc.vector.tensor_tensor(xTl[:], ps[:, 6:8, :], xTh[:].bitcast(F32),
                                                ALU.subtract).then_inc(v_xTl, 1)
                    if has(i):
                        dve.wait_ge(a_exp, i + 1)
                        nc.vector.tensor_reduce(ssum[:], PR[:].rearrange("p t h j -> p (t h) j"), AX.X,
                                                ALU.add).then_inc(v_sum, 1)
                        dve.wait_ge(v_sum, i + 1)
                        nc.vector.reciprocal(srec[:], ssum[:]).then_inc(v_rec, 1)
                    if has(i + 2):
                        dve.wait_ge(g_rs1, i + 3)
                        if has(i + 1):
                            dve.wait_ge(p_xT, i + 2)
                        normalise(XB[:, u], mv1, rs1, XN, v_xn)
                    if has(i - 3):
                        dve.wait_ge(a_gexp, n + 1)
                        nc.vector.tensor_reduce(gsum[:], gexp[:], AX.X, ALU.add).then_inc(v_gsum, 1)
                        dve.wait_ge(v_gsum, n + 1)
                        nc.vector.reciprocal(grec[:], gsum[:]).then_inc(v_grec, 1)
                        dve.wait_ge(v_grec, n + 1)
                        b, pair = n // (NBLK // B), n % (NBLK // B) if isinstance(n, int) else n & (NBLK // B - 1)
                        flat = probs[:].rearrange("p b e t -> p (b e t)")
                        for t in range(TPB):
                            at = b * (E * NT) + pair * TPB + t
                            last = nc.vector.tensor_scalar(flat[:, bass.ds(at, E, step=NT)], gexp[:, t, :],
                                                           grec[:, t:t + 1], None, ALU.mult)
                        last.then_inc(v_gate, 1)
                steps(dve, step)

            @block.tensor
            def _(pe):
                def three(psum, pairs, **kw):
                    n = len(pairs)
                    for k, (wh, wl, mh, ml) in enumerate(pairs):
                        nc.tensor.matmul(psum, wh, mh, start=(k == 0), stop=False, **kw)
                        nc.tensor.matmul(psum, wh, ml, start=False, stop=False, **kw)
                        last = nc.tensor.matmul(psum, wl, mh, start=False, stop=(k == n - 1), **kw)
                    return last

                def step(i, u, half, has):
                    if has(i - 1):
                        pe.wait_ge(g_prob, i)
                        if has(i - 3):
                            pe.wait_ge(a_xn2T, i - 2)
                        elif has(i):
                            pe.wait_ge(v_xTl, i + 1)
                        if has(i - 4):
                            pe.wait_ge(v_gsub, i - 3)
                        flat = PR[:].rearrange("p t h j -> p (t h j)")
                        for t in range(TPB):
                            for c, (at, n) in enumerate(CH):
                                dst = tails[:, t, :] if c == NCH - 1 else ps[:, 6 + t, at:at + P]
                                last = nc.tensor.transpose(dst, flat[:, t * HJ + at:t * HJ + at + n], ident[:])
                        last.then_inc(p_pT, 1)
                    if has(i):
                        pe.wait_ge(v_xTl, i + 1)
                        if isinstance(i, int):
                            batch = i // (NBLK // B)
                            at = [batch * KD * HJ + dk * HJ for dk in range(KD)]
                        else:
                            base = pe.snap(i // (NBLK // B) * (KD * HJ))
                            at = [base + dk * HJ for dk in range(KD)]
                        fh, fl = (m[:].rearrange("p b k n -> p (b k n)") for m in (AH, AL))
                        for t in range(TPB):
                            for part, (c0, n) in enumerate(((0, MAIN), (MAIN, REST))):
                                last = three(scores(t, part),
                                             [(xTh[:, t, dk * P:(dk + 1) * P], xTl[:, t, dk * P:(dk + 1) * P],
                                               fh[:, bass.ds(at[dk] + c0, n)], fl[:, bass.ds(at[dk] + c0, n)])
                                              for dk in range(KD)])
                        last.then_inc(p_s, 1)
                    if has(i - 3):
                        pe.wait_ge(a_xn2T, i - 2)
                        if has(i - 1):
                            pe.wait_ge(v_pTl, i)
                        for t in range(TPB):
                            for dk in range(KD):
                                last = nc.tensor.matmul(gate_sc[:, t, :], xn2T[:, t, dk * P:(dk + 1) * P], gwT[:, dk, :],
                                                        start=(dk == 0), stop=(dk == KD - 1))
                        last.then_inc(p_g, 1)
                    if has(i + 1):
                        pe.wait_ge(v_xn, i + 2)
                        if has(i - 1):
                            pe.wait_ge(v_pTl, i)
                        for t in range(TPB):
                            for dk in range(KD):
                                last = nc.tensor.transpose(ps[:, 6 + t, dk * P:(dk + 1) * P],
                                                           XN[:, t, dk * P:(dk + 1) * P], ident[:])
                        last.then_inc(p_xT, 1)
                    if has(i - 1):
                        pe.wait_ge(v_pTl, i)
                        if has(i - 2):
                            pe.wait_ge(v_x1, i - 1)
                        n = i - 1
                        if isinstance(n, int):
                            batch = n // (NBLK // B)
                            at = [(batch * NCH + c) * D for c in range(NCH)]
                        else:
                            base = pe.snap(n // (NBLK // B) * (NCH * D))
                            at = [base + c * D for c in range(NCH)]
                        fh, fl = (m[:].rearrange("p b k n -> p (b k n)") for m in (BH, BL))
                        for t in range(TPB):
                            last = three(ps[:, 4 + t, :],
                                         [(pTh[0:k, t, c, :], pTl[0:k, t, c, :],
                                           fh[0:k, bass.ds(at[c], D)], fl[0:k, bass.ds(at[c], D)])
                                          for c, (_, k) in enumerate(CH)])
                        last.then_inc(p_o, 1)
                    if has(i - 2):
                        pe.wait_ge(v_xn2, i - 1)
                        if has(i + 1):
                            pe.wait_ge(v_xTl, i + 2)
                        for t in range(TPB):
                            for dk in range(KD):
                                last = nc.tensor.transpose(ps[:, 6 + t, dk * P:(dk + 1) * P],
                                                           XN2[:, u, t, dk * P:(dk + 1) * P], ident[:])
                        last.then_inc(p_xn2T, 1)
                steps(pe, step)
        tiles.close()
        attn.close()

        pick = ExitStack()
        thr = sb(pick, "thr", [P, COLS])
        cand = sb(pick, "cand", [P, COLS])
        bit = sb(pick, "bit", [P, COLS])
        kept = sb(pick, "kept", [P, COLS])
        hit = sb(pick, "hit", [P, COLS, NT], BF16)
        cnt = sb(pick, "cnt", [P, COLS], BF16)
        above = sb(pick, "above", [P, COLS, NT], BF16)
        tied = sb(pick, "tied", [P, COLS, NT], BF16)
        chosen = sb(pick, "chosen", [P, COLS, NT], BF16)
        room = sb(pick, "room", [P, COLS])
        chain = sb(pick, "chain", [P, COLS, NT])
        run = sb(pick, "run", [P, COLS, NT])
        run2 = sb(pick, "run2", [P, COLS, NT])
        place = sb(pick, "place", [P, COLS, NT])
        q1 = sb(pick, "q1", [P, COLS, NT])
        q2 = sb(pick, "q2", [P, COLS, NT])
        quarter = sb(pick, "quarter", [P, COLS, NT])
        row = sb(pick, "row", [P, COLS, NT])
        rest1 = sb(pick, "rest1", [P, COLS, NT])
        rest2 = sb(pick, "rest2", [P, COLS, NT])
        gp = [sb(pick, f"gp{i}", [P, COLS, NT], BF16) for i in range(3)]
        inq = sb(pick, "inq", [P, COLS, NT, CT], BF16)
        vals = sb(pick, "vals", [P, COLS, NT, NV, CT], BF16)
        hot = sb(pick, "hot", [P, 2, NT, P], BF16)
        found = sb(pick, "found", [P, COLS, NV, CT])
        fsum = sb(pick, "fsum", [P, COLS, CT])

        BITS = 30
        t_init = sem("t_init")
        t_cand, t_hit, t_cnt, t_tot, t_kept, t_thr, t_bit = (sem(f"t_{n}") for n in
                                                             "cand hit cnt tot kept thr bit".split())
        c_dve = sem("c_dve")
        c_pe = sem("c_pe")
        h_hot = sem("h_hot")
        h_used = sem("h_used")

        def u32(t):
            return t[:].bitcast(U32)

        def spread(t):
            return t[:].unsqueeze(2).broadcast_to([P, COLS, NT])

        prob3 = probs[:].rearrange("p b e t -> p (b e) t")

        with nc.Block() as block:
            @block.tensor
            def _(pe):
                with pe.Fori(0, BITS, 1) as k:
                    pe.wait_ge(t_cnt, k + 1)
                    nc.tensor.matmul(ps[:, 0, 0:COLS], ones_bf[:], cnt[:], start=True, stop=True).then_inc(t_tot, 1)
                pe.wait_ge(c_dve, 1)
                nc.tensor.matmul(ps[:, 0, 0:COLS], ones_bf[:], cnt[:], start=True, stop=True).then_inc(c_pe, 1)
                for m, mask in ((1, tied), (2, chosen)):
                    pe.wait_ge(c_dve, m + 1)
                    flat = mask[:].rearrange("p c t -> p (c t)")
                    nc.tensor.matmul(ps[:, 1, 0:COLS * NT], before_bf[:], flat, start=True, stop=True)
                    nc.tensor.matmul(ps[:, 2, 0:COLS * NT], ones_bf[:], flat, start=True, stop=True).then_inc(c_pe, 1)
                pe.wait_ge(c_dve, 4)
                flat = vals[:].rearrange("p c t v q -> p (c t v q)")
                with pe.Fori(0, COLS // 2, 1) as k:
                    for u in range(2):
                        pe.wait_ge(h_hot, 2 * k + u + 1)
                        for t in range(NT):
                            last = nc.tensor.matmul(ps[:, 3, bass.ds((2 * k + u) * (NV * CT), NV * CT)], hot[:, u, t, :],
                                                    flat[:, bass.ds((2 * k + u) * (NT * NV * CT) + t * NV * CT, NV * CT)],
                                                    start=(t == 0), stop=(t == NT - 1))
                        last.then_inc(h_used, 1)

            @block.vector
            def _(dve):
                done = [0]

                def link(ins):
                    done[0] += 1
                    ins.then_inc(t_init, 1)
                    dve.wait_ge(t_init, done[0])

                nc.vector.memset(chain[:], 1.0)
                nc.vector.memset(thr[:], 0.0)
                link(nc.vector.memset(bit[:], 2.0 ** -63))
                link(nc.vector.memset(chain[:, :, 0:1], 0.0))
                with dve.Fori(0, BITS, 1) as k:
                    nc.vector.tensor_tensor(u32(cand), u32(thr), u32(bit), ALU.bitwise_or).then_inc(t_cand, 1)
                    dve.wait_ge(t_cand, k + 1)
                    nc.vector.tensor_tensor(hit[:], prob3, spread(cand), ALU.is_ge).then_inc(t_hit, 1)
                    nc.vector.tensor_scalar(u32(bit), u32(bit), 1, None, ALU.logical_shift_right).then_inc(t_bit, 1)
                    dve.wait_ge(t_hit, k + 1)
                    with nc.allow_low_precision(reason="counts up to 16 are exact in bfloat16"):
                        nc.vector.tensor_reduce(cnt[:], hit[:], AX.X, ALU.add).then_inc(t_cnt, 1)
                    dve.wait_ge(t_tot, k + 1)
                    nc.vector.scalar_tensor_tensor(out=kept[:], in0=ps[:, 0, 0:COLS], scalar=float(CAP), in1=cand[:],
                                                   op0=ALU.is_ge, op1=ALU.mult).then_inc(t_kept, 1)
                    dve.wait_ge(t_kept, k + 1)
                    nc.vector.tensor_tensor(thr[:], thr[:], kept[:], ALU.max).then_inc(t_thr, 1)
                    dve.wait_ge(t_thr, k + 1)
                link(nc.vector.tensor_tensor(above[:], prob3, spread(thr), ALU.is_gt))
                nc.vector.tensor_tensor(tied[:], prob3, spread(thr), ALU.is_equal)
                with nc.allow_low_precision(reason="counts up to 16 are exact in bfloat16"):
                    nc.vector.tensor_reduce(cnt[:], above[:], AX.X, ALU.add).then_inc(c_dve, 2)
                dve.wait_ge(c_pe, 1)
                link(nc.vector.tensor_scalar(room[:], ps[:, 0, 0:COLS], -1.0, float(CAP), ALU.mult, ALU.add))

                def places(m):
                    dve.wait_ge(c_pe, m)
                    inside = ps[:, 1, 0:COLS * NT].rearrange("p (c t) -> p c t", t=NT)
                    sums = ps[:, 2, 0:COLS * NT].rearrange("p (c t) -> p c t", t=NT)
                    link(nc.vector.tensor_tensor_scan(run[:].rearrange("p c t -> p (c t)"),
                                                      chain[:].rearrange("p c t -> p (c t)"),
                                                      ps[:, 2, 0:COLS * NT], 0.0, ALU.mult, ALU.add))
                    link(nc.vector.tensor_tensor(run2[:], run[:], sums, ALU.subtract))
                    link(nc.vector.tensor_tensor(place[:], run2[:], inside, ALU.add))

                places(2)
                link(nc.vector.tensor_tensor(q1[:], place[:], spread(room), ALU.is_lt))
                link(nc.vector.tensor_tensor(q2[:], q1[:], tied[:], ALU.mult))
                nc.vector.tensor_tensor(chosen[:], q2[:], above[:], ALU.add).then_inc(c_dve, 1)
                link(nc.vector.tensor_copy(gp[0][:], prob3))
                link(nc.vector.tensor_tensor(rest1[:], prob3, gp[0][:], ALU.subtract))
                link(nc.vector.tensor_copy(gp[1][:], rest1[:]))
                link(nc.vector.tensor_tensor(rest2[:], rest1[:], gp[1][:], ALU.subtract))
                link(nc.vector.tensor_copy(gp[2][:], rest2[:]))
                places(3)
                link(nc.vector.tensor_scalar(q1[:], place[:], float(P), None, ALU.is_ge))
                link(nc.vector.scalar_tensor_tensor(out=q2[:], in0=place[:], scalar=float(2 * P), in1=q1[:],
                                                    op0=ALU.is_ge, op1=ALU.add))
                link(nc.vector.scalar_tensor_tensor(out=quarter[:], in0=place[:], scalar=float(3 * P), in1=q2[:],
                                                    op0=ALU.is_ge, op1=ALU.add))
                link(nc.vector.scalar_tensor_tensor(out=q1[:], in0=quarter[:], scalar=float(-P), in1=place[:],
                                                    op0=ALU.mult, op1=ALU.add))
                link(nc.vector.scalar_tensor_tensor(out=q2[:], in0=q1[:], scalar=1.0, in1=chosen[:],
                                                    op0=ALU.add, op1=ALU.mult))
                nc.vector.tensor_scalar(row[:], q2[:], -1.0, None, ALU.add)
                flat4 = [P, COLS * NT, CT]

                def each(t):
                    return t.unsqueeze(2).broadcast_to(flat4)

                link(nc.vector.tensor_tensor(inq[:].rearrange("p c t q -> p (c t) q"),
                                             each(quarter[:].rearrange("p c t -> p (c t)")),
                                             quarter_iota[:].unsqueeze(1).broadcast_to(flat4), ALU.is_equal))
                numbers = [part_iota[:].broadcast_to([P, COLS * NT]), tile_iota[:].rearrange("p b e t -> p (b e t)"),
                           *(g[:].rearrange("p c t -> p (c t)") for g in gp)]
                for v, number in enumerate(numbers):
                    last = nc.vector.tensor_tensor(vals[:, :, :, v, :].rearrange("p c t q -> p (c t) q"),
                                                   inq[:].rearrange("p c t q -> p (c t) q"), each(number), ALU.mult)
                last.then_inc(c_dve, 1)
                rows = row[:].rearrange("p c t -> p (c t)")
                one_hot = [P, NT, P]

                def column(c, u):
                    nc.vector.tensor_tensor(hot[:, u], rows[:, bass.ds(c * NT, NT)].unsqueeze(2).broadcast_to(one_hot),
                                            col_iota[:].unsqueeze(1).broadcast_to(one_hot),
                                            ALU.is_equal).then_inc(h_hot, 1)

                for c in range(2):
                    column(c, c)
                with dve.Fori(1, COLS // 2, 1) as k:
                    for u in range(2):
                        dve.wait_ge(h_used, 2 * k + u - 1)
                        column(2 * k + u, u)
                dve.wait_ge(h_used, COLS)
                link(nc.vector.tensor_copy(found[:].rearrange("p c v q -> p (c v q)"), ps[:, 3, 0:COLS * NV * CT]))
                nc.vector.scalar_tensor_tensor(out=tok_idx[:], in0=found[:, :, 1, :], scalar=float(P),
                                               in1=found[:, :, 0, :], op0=ALU.mult, op1=ALU.add)
                link(nc.vector.tensor_tensor(fsum[:], found[:, :, 2, :], found[:, :, 3, :], ALU.add))
                nc.vector.tensor_tensor(tok_gate[:], fsum[:], found[:, :, 4, :], ALU.add)
        pick.close()

        ffn = ExitStack()
        G, GF = 4, KF // 4
        SLOTS1, SLOTS2 = 4, 8
        w1_raw = sb(ffn, "w1_raw", [P, 2, KD, GF * P])
        w2_raw = sb(ffn, "w2_raw", [P, 2, GF, D])
        w1h = sb(ffn, "w1h", [P, SLOTS1, KD, P], F32R)
        w1l = sb(ffn, "w1l", [P, SLOTS1, KD, P], F32R)
        w2h = sb(ffn, "w2h", [P, SLOTS2, D], F32R)
        w2l = sb(ffn, "w2l", [P, SLOTS2, D], F32R)
        eTh = sb(ffn, "eTh", [P, 2, KD, CAP], F32R)
        eTl = sb(ffn, "eTl", [P, 2, KD, CAP], F32R)
        hf = sb(ffn, "hf", [P, 2, CAP])
        hh = sb(ffn, "hh", [P, 4, CAP], F32R)
        hl = sb(ffn, "hl", [P, 4, CAP], F32R)
        rows_in = sb(ffn, "rows_in", [P, CT, D])
        Y = sb(ffn, "Y", [P, CT, D])
        gidx = sb(ffn, "gidx", [P, CT], U32)
        sidx = sb(ffn, "sidx", [P, CT], U32)

        f_raw = [sem(f"f_raw{i}") for i in range(2)]
        f_hh = sem("f_hh")
        f_passed = sem("f_passed")
        (f_w1h, f_w2h, f_w1l, f_w2l, f_up, f_gelu, f_h, f_down, f_gidx, f_sidx, f_tr, f_eTh, f_eTl, f_ya, f_yd,
         f_yfree) = (sem(f"f_{n}") for n in
                     "w1h w2h w1l w2l up gelu h down gidx sidx tr eTh eTl ya yd yfree".split())
        f_rows = sem("f_rows")
        f_scat = sem("f_scat")
        flat_idx = tok_idx[:].rearrange("p c q -> p (c q)")
        flat_gate = tok_gate[:].rearrange("p c q -> p (c q)")
        w1_g = w1.rearrange("e (k p) f -> e p k f", p=P)
        w2_g = w2.rearrange("e (k p) d -> e p k d", p=P)
        flat_eTh = eTh[:].rearrange("p b k n -> p (b k n)")
        flat_eTl = eTl[:].rearrange("p b k n -> p (b k n)")
        EB = KD * CAP

        def passed(eng, sem, value):
            eng.wait_ge(sem, value)
            eng.sem_inc(f_passed, 1)

        def looped(eng, body):
            with eng.Fori(0, COLS - 1, 1) as i:
                body(i, True)
            body(COLS - 1, False)

        with nc.Block() as block:
            @block.sync
            def _(sp):
                def group(i, e, g, wait):
                    a, b = w1_g[e, :, :, g * GF * P:(g + 1) * GF * P], w2_g[e, :, g * GF:(g + 1) * GF, :]
                    if wait:
                        passed(sp, f_w2l, i * KF + (g - 1) * GF)
                    sp.dma_start(w1_raw[:, g % 2], a).then_inc(f_raw[g % 2], 16)
                    sp.dma_start(w2_raw[:, g % 2], b).then_inc(f_raw[g % 2], 16)

                for g in range(G):
                    group(0, 0, g, g >= 2)
                with sp.Fori(1, COLS, 1) as i:
                    for g in range(G):
                        group(i, i & (E - 1), g, True)

            @block.gpsimd
            def _(pool):
                def gather(i, first):
                    if not first:
                        passed(pool, f_rows, i * CT * 16)
                    pool.tensor_copy(gidx[:], flat_idx[:, bass.ds(i * CT, CT)]).then_inc(f_gidx, 1)
                    passed(pool, f_gidx, i + 1)
                    if not first:
                        passed(pool, f_tr, i * KD)
                    for c in range(CT):
                        pool.indirect_dma_start(out=rows_in[:, c, :], out_offset=None, in_=xn2_rows,
                                                in_offset=bass.IndirectOffsetOnAxis(ap=gidx[:, c:c + 1], axis=0),
                                                ).then_inc(f_rows, 16)

                def body(i, more):
                    if more:
                        gather(i + 1, False)
                    pool.tensor_copy(sidx[:], flat_idx[:, bass.ds(i * CT, CT)]).then_inc(f_sidx, 1)
                    passed(pool, f_sidx, i + 1)
                    passed(pool, f_ya, i + 1)
                    passed(pool, f_yd, i + 1)
                    for c in range(CT):
                        pool.indirect_dma_start(out=out_rows,
                                                out_offset=bass.IndirectOffsetOnAxis(ap=sidx[:, c:c + 1], axis=0),
                                                in_=Y[:, c, :], in_offset=None, compute_op=ALU.add,
                                                ).then_inc(f_scat, 16)
                        passed(pool, f_scat, (i * CT + c + 1) * 16)
                    pool.sem_inc(f_yfree, 1)

                gather(0, True)
                looped(pool, body)

            @block.scalar
            def _(act):
                def weights(i, f, wait1, wait2):
                    g, j = divmod(f, GF)
                    if j == 0:
                        act.wait_ge(f_raw[g % 2], 64 * i + 32 * (g // 2 + 1))
                    if wait1 is not None:
                        act.wait_ge(f_up, wait1)
                    nc.scalar.activation(w1h[:, f % SLOTS1], w1_raw[:, g % 2, :, j * P:(j + 1) * P],
                                         ACT.Copy).then_inc(f_w1h, 1)
                    if wait2 is not None:
                        act.wait_ge(f_down, wait2)
                    nc.scalar.activation(w2h[:, f % SLOTS2], w2_raw[:, g % 2, j, :], ACT.Copy).then_inc(f_w2h, 1)

                def token_chunk(i, k):
                    act.wait_ge(f_tr, i * KD + k + 1)
                    half = (i & 1) * EB
                    nc.scalar.activation(flat_eTh[:, bass.ds(half + k * CAP, CAP)], ps[:, 6 + k % 2, :],
                                         ACT.Copy).then_inc(f_eTh, 1)

                def body(i, more):
                    for f in range(KF):
                        if f + 2 < KF:
                            weights(i, f + 2, i * KF + f - 1 if f >= 2 else None,
                                    i * KF + f - 5 if f >= 6 else None)
                        elif more:
                            weights(i + 1, f + 2 - KF, i * KF + f - 1, i * KF + f - 5)
                        act.wait_ge(f_up, i * KF + f + 1)
                        if f >= 2:
                            act.wait_ge(f_h, i * KF + f - 1)
                        nc.scalar.activation(hf[:, f % 2, :], ps[:, 4 + f % 2, :], ACT.Gelu).then_inc(f_gelu, 1)
                        if more and 9 <= f < 9 + KD:
                            token_chunk(i + 1, f - 9)
                    act.wait_ge(f_down, (i + 1) * KF)
                    act.wait_ge(f_yfree, i + 1)
                    for c in range(CT // 2, CT):
                        last = nc.scalar.activation(Y[:, c, :], ps[:, c, :], ACT.Copy,
                                                    scale=flat_gate[:, bass.ds(i * CT + c, 1)])
                    last.then_inc(f_ya, 1)

                for f in range(2):
                    weights(0, f, None, None)
                for k in range(KD):
                    token_chunk(0, k)
                looped(act, body)

            @block.vector
            def _(dve):
                def weights(f, n):
                    g, j = divmod(f, GF)
                    dve.wait_ge(f_w1h, n + 1)
                    nc.vector.tensor_tensor(w1l[:, f % SLOTS1], w1_raw[:, g % 2, :, j * P:(j + 1) * P],
                                            w1h[:, f % SLOTS1].bitcast(F32), ALU.subtract).then_inc(f_w1l, 1)
                    dve.wait_ge(f_w2h, n + 1)
                    nc.vector.tensor_tensor(w2l[:, f % SLOTS2], w2_raw[:, g % 2, j, :],
                                            w2h[:, f % SLOTS2].bitcast(F32), ALU.subtract).then_inc(f_w2l, 1)

                def token_chunk(i, k):
                    dve.wait_ge(f_eTh, i * KD + k + 1)
                    at = bass.ds((i & 1) * EB + k * CAP, CAP)
                    nc.vector.tensor_tensor(flat_eTl[:, at], ps[:, 6 + k % 2, :], flat_eTh[:, at].bitcast(F32),
                                            ALU.subtract).then_inc(f_eTl, 1)

                def body(i, more):
                    for f in range(KF):
                        if f + 2 < KF or more:
                            weights((f + 2) % KF, i * KF + f + 2)
                        dve.wait_ge(f_gelu, i * KF + f + 1)
                        if f >= 4:
                            dve.wait_ge(f_down, i * KF + f - 3)
                        nc.vector.tensor_copy(hh[:, f % 4], hf[:, f % 2, :]).then_inc(f_hh, 1)
                        dve.wait_ge(f_hh, i * KF + f + 1)
                        nc.vector.tensor_tensor(hl[:, f % 4], hf[:, f % 2, :], hh[:, f % 4].bitcast(F32),
                                                ALU.subtract).then_inc(f_h, 1)
                        if more and 9 <= f < 9 + KD:
                            token_chunk(i + 1, f - 9)
                    dve.wait_ge(f_down, (i + 1) * KF)
                    dve.wait_ge(f_yfree, i + 1)
                    for c in range(CT // 2):
                        last = nc.vector.tensor_scalar(Y[:, c, :], ps[:, c, :], flat_gate[:, bass.ds(i * CT + c, 1)],
                                                       None, ALU.mult)
                    last.then_inc(f_yd, 1)

                dve.sem_inc(f_yfree, 1)
                for f in range(2):
                    weights(f, f)
                for k in range(KD):
                    token_chunk(0, k)
                looped(dve, body)

            @block.tensor
            def _(pe):
                def transposes(i, k, first):
                    if k == 0:
                        pe.wait_ge(f_rows, 16 * CT * (i + 1))
                    if not (first and k < 2):
                        pe.wait_ge(f_eTl, i * KD + k - 1)
                    for c in range(CT):
                        last = nc.tensor.transpose(ps[:, 6 + k % 2, c * P:(c + 1) * P],
                                                   rows_in[:, c, k * P:(k + 1) * P], ident[:])
                    last.then_inc(f_tr, 1)

                def up(i, f):
                    pe.wait_ge(f_w1l, i * KF + f + 1)
                    if f == 0:
                        pe.wait_ge(f_eTl, (i + 1) * KD)
                    if f >= 2:
                        pe.wait_ge(f_gelu, i * KF + f - 1)
                    for k in range(KD):
                        at = bass.ds(halves[0] + k * CAP, CAP)
                        wh, wl = w1h[:, f % SLOTS1, k, :], w1l[:, f % SLOTS1, k, :]
                        nc.tensor.matmul(ps[:, 4 + f % 2, :], wh, flat_eTh[:, at], start=(k == 0), stop=False)
                        nc.tensor.matmul(ps[:, 4 + f % 2, :], wh, flat_eTl[:, at], start=False, stop=False)
                        last = nc.tensor.matmul(ps[:, 4 + f % 2, :], wl, flat_eTh[:, at], start=False,
                                                stop=(k == KD - 1))
                    last.then_inc(f_up, 1)

                def down(i, f):
                    pe.wait_ge(f_h, i * KF + f + 1)
                    pe.wait_ge(f_w2l, i * KF + f + 1)
                    for c in range(CT):
                        th, tl = (t[:, f % 4, c * P:(c + 1) * P] for t in (hh, hl))
                        wh, wl = w2h[:, f % SLOTS2, :], w2l[:, f % SLOTS2, :]
                        nc.tensor.matmul(ps[:, c, :], th, wh, start=(f == 0), stop=False)
                        nc.tensor.matmul(ps[:, c, :], th, wl, start=False, stop=False)
                        last = nc.tensor.matmul(ps[:, c, :], tl, wh, start=False, stop=(f == KF - 1))
                    last.then_inc(f_down, 1)

                halves = [0]

                def body(i, more):
                    halves[0] = pe.snap((i & 1) * EB) if more else (i & 1) * EB
                    for f in range(KF):
                        up(i, f)
                        if f >= 2:
                            down(i, f - 2)
                        if more and 8 <= f < 8 + KD:
                            transposes(i + 1, f - 8, False)
                    for f in range(KF - 2, KF):
                        down(i, f)

                for k in range(KD):
                    transposes(0, k, True)
                looped(pe, body)
        ffn.close()


_INS = ['x', 'ctx_768', 'L0_xattn_Wq', 'L0_xattn_Wk', 'L0_xattn_Wv', 'L0_xattn_Wo', 'L0_xattn_bo', 'L0_ffn_gate_w',
        'L0_ffn_w1', 'L0_ffn_w2']


def kernel(**inputs):
    import numpy as _np
    import concourse.bacc as _bacc
    from concourse import mybir as _mybir
    from concourse.bass_utils import run_bass_kernel_spmd as _run

    nc = _bacc.Bacc("TRN2", target_bir_lowering=False, num_devices=1)
    arrays, args = {}, []
    for name in _INS:
        a = _np.ascontiguousarray(inputs[name])
        arrays[f"in_{name}_dram"] = a
        args.append(nc.dram_tensor(f"in_{name}_dram", a.shape, _mybir.dt.from_np(a.dtype), kind="ExternalInput").ap())
    out = nc.dram_tensor("out_dram", (B, S, D), _mybir.dt.float32, kind="ExternalOutput").ap()
    xattn_expert_choice(nc, *args, out)
    r = _run(nc, [arrays], core_ids=[0])
    return r.results[0]["out_dram"]
```

```python
import concourse.bass as bass
from concourse import mybir
from concourse.alu_op_type import AluOpType as ALU
from contextlib import ExitStack

F32 = mybir.dt.float32
F32R = mybir.dt.float32r
BF16 = mybir.dt.bfloat16
U32 = mybir.dt.uint32
ACT = mybir.ActivationFunctionType
AX = mybir.AxisListType

P = 128
B, S, D = 2, 2048, 512
H, HD = 8, 64
J, CK = 77, 384
E, F = 8, 2048
CAP = 2 * S // E
KD, KC, KF = D // P, CK // P, F // P
HJ = H * J
HALF = HJ // 2
MAIN, REST = 6 * J, 2 * J
PAIR = 2 * J
CH = [(c * P, min(P, HJ - c * P)) for c in range(-(-HJ // P))]
NCH = len(CH)
WC = NCH * P
TPB = 2
NT = S // P
NBLK = B * NT // TPB
COLS = B * E
CT = CAP // P
EPS = 1e-5
CAND = 3
ROUNDS = 15
NV = 5


def xattn_expert_choice(nc, x, ctx, wq, wk, wv, wo, bo, gate_w, w1, w2, out):
    xn2_rows = nc.dram_tensor("xn2_rows", (B * S, D), F32, kind="Internal").ap()
    x_blk = x.rearrange("b (n t p) d -> (b n) p t d", t=TPB, p=P)
    out_blk = out.rearrange("b (n t p) d -> (b n) p t d", t=TPB, p=P)
    out_rows = out.rearrange("b s d -> (b s) d")
    xn2_blk = xn2_rows.rearrange("(n t p) d -> n p t d", t=TPB, p=P)

    top = ExitStack()
    with top:
        def sb(scope, name, shape, dt=F32):
            return scope.enter_context(nc.sbuf_tensor(name, shape, dt))

        def sem(name):
            return top.enter_context(nc.semaphore(name))

        ident = sb(top, "ident", [P, P])
        ones_bf = sb(top, "ones_bf", [P, P], BF16)
        before_bf = sb(top, "before_bf", [P, P], BF16)
        col_iota = sb(top, "col_iota", [P, P], BF16)
        quarter_iota = sb(top, "quarter_iota", [P, CT], BF16)
        part_iota = sb(top, "part_iota", [P, 1], BF16)
        tile_iota = sb(top, "tile_iota", [P, B, E, NT], BF16)
        eps_c = sb(top, "eps_c", [P, TPB])
        pow_c = sb(top, "pow_c", [P, TPB])
        minus_c = sb(top, "minus_c", [P, TPB])
        bo_rows = sb(top, "bo_rows", [P, TPB, D])
        gwT = sb(top, "gwT", [P, KD, E])
        probs = sb(top, "probs", [P, B, E, NT])
        tok_idx = sb(top, "tok_idx", [P, COLS, CT], U32)
        tok_gate = sb(top, "tok_gate", [P, COLS, CT])
        XB = sb(top, "XB", [P, 2, TPB, D])
        rows_in = XB[:].rearrange("p b t d -> p (b t) d")
        assert 2 * TPB == CT
        ps = top.enter_context(nc.psum_tensor("ps", [P, 8, 512], F32))
        thr = sb(top, "thr", [P, E])
        cand = sb(top, "cand", [P, E, CAND])
        bits = sb(top, "bits", [P, E, CAND])
        kept = sb(top, "kept", [P, E, CAND])
        best = sb(top, "best", [P, E])
        hit = sb(top, "hit", [P, E, CAND, NT], BF16)
        cnt = sb(top, "cnt", [P, E * CAND], BF16)
        above = sb(top, "above", [P, E, NT], BF16)
        tied = sb(top, "tied", [P, E, NT], BF16)
        chosen = sb(top, "chosen", [P, E, NT], BF16)
        room = sb(top, "room", [P, E])
        chain = sb(top, "chain", [P, E, NT])
        run = sb(top, "run", [P, E, NT])
        run2 = sb(top, "run2", [P, E, NT])
        place = sb(top, "place", [P, E, NT])
        q1 = sb(top, "q1", [P, E, NT])
        q2 = sb(top, "q2", [P, E, NT])
        quarter = sb(top, "quarter", [P, E, NT])
        row = sb(top, "row", [P, B, E, NT])
        rest1 = sb(top, "rest1", [P, E, NT])
        rest2 = sb(top, "rest2", [P, E, NT])
        gp = [sb(top, f"gp{i}", [P, E, NT], BF16) for i in range(3)]
        inq = sb(top, "inq", [P, E, NT, CT], BF16)
        vals = sb(top, "vals", [P, B, E, NT, NV, CT], BF16)
        hot = sb(top, "hot", [P, NT, P], BF16)
        found = sb(top, "found", [P, NV, CT])
        fsum = sb(top, "fsum", [P, CT])
        G, GF = 4, KF // 4
        gidx = sb(top, "gidx", [P, CT], U32)
        sidx = sb(top, "sidx", [P, CT], U32)
        w1_raw = sb(top, "w1_raw", [P, 2, KD, GF * P])
        w2_raw = sb(top, "w2_raw", [P, 2, GF, D])

        attn = ExitStack()
        AH = sb(attn, "AH", [P, B, KD, HJ], F32R)
        AL = sb(attn, "AL", [P, B, KD, HJ], F32R)
        BH = sb(attn, "BH", [P, B, NCH, D], F32R)
        BL = sb(attn, "BL", [P, B, NCH, D], F32R)
        init = ExitStack()
        ctx_sb = sb(init, "ctx_sb", [J, B, CK])
        gw_sb = sb(init, "gw_sb", [E, D])
        wq_sb = w1_raw[:, 1]
        wk_sb = sb(init, "wk_sb", [P, KC, D])
        wv_sb = sb(init, "wv_sb", [P, KC, D])
        wo_sb = w1_raw[:, 0]
        ctxT = sb(init, "ctxT", [P, KC, B, J])
        wqT = sb(init, "wqT", [P, KD, D])
        kx = sb(init, "kx", [P, B, KD, PAIR])
        vx = sb(init, "vx", [P, B, KD, WC])
        before_f = sb(init, "before_f", [P, P])

        c_ident = sem("c_ident")
        c_zero = sem("c_zero")
        c_const = sem("c_const")
        d_ctx, d_gw, d_wk, d_wv, d_wq, d_wo, d_bo = (sem(f"d_{n}") for n in "ctx gw wk wv wq wo bo".split())
        p_ctxT = sem("p_ctxT")
        e_ctxT = sem("e_ctxT")
        p_kv = sem("p_kv")
        e_kv = sem("e_kv")
        p_wqT = sem("p_wqT")
        e_wqT = sem("e_wqT")
        p_fold = sem("p_fold")
        e_hi = sem("e_hi")
        e_lo = sem("e_lo")

        folds = [("A", b, dk) for b in range(B) for dk in range(KD)] + [("B", b, c) for b in range(B) for c in range(NCH)]

        def fold_bufs(n):
            kind, b, c = folds[n]
            pair = ps[:, 2 * (n % 4):2 * (n % 4) + 2, :]
            if kind == "A":
                src = pair[:, :, 0:HALF]
                hi, lo = (t[:, b, c, :].rearrange("p (h j) -> p h j", h=2) for t in (AH, AL))
            else:
                src = pair[:, 0, :]
                hi, lo = BH[:, b, c, :], BL[:, b, c, :]
            return src, hi, lo

        with nc.Block() as block:
            @block.sync
            def _(sp):
                sp.dma_start(ctx_sb[:], ctx.rearrange("b j c -> j b c")).then_inc(d_ctx, 16)
                sp.dma_start(gw_sb[:], gate_w).then_inc(d_gw, 16)
                sp.dma_start(wk_sb[:], wk.rearrange("(c p) n -> p c n", p=P)).then_inc(d_wk, 16)
                sp.dma_start(wv_sb[:], wv.rearrange("(c p) n -> p c n", p=P)).then_inc(d_wv, 16)
                sp.dma_start(wq_sb, wq.rearrange("(c p) n -> p c n", p=P)).then_inc(d_wq, 16)
                sp.dma_start(wo_sb, wo.rearrange("(c p) n -> p c n", p=P)).then_inc(d_wo, 16)
                for t in range(TPB):
                    sp.dma_start(bo_rows[:, t, :], bo.partition_broadcast(P)).then_inc(d_bo, 16)
                sp.wait_ge(d_bo, 16 * TPB)

            @block.gpsimd
            def _(pool):
                pool.memset(ident[:], 0.0).then_inc(c_zero, 1)
                pool.wait_ge(c_zero, 1)
                pool.affine_select(out=ident[:], in_=ident[:], compare_op=ALU.not_equal, fill=1.0, base=0,
                                   pattern=[[-1, P]], channel_multiplier=1).then_inc(c_ident, 1)
                pool.memset(before_f[:], 1.0).then_inc(c_zero, 1)
                pool.wait_ge(c_zero, 2)
                pool.affine_select(out=before_bf[:], in_=before_f[:], compare_op=ALU.is_gt, fill=0.0, base=0,
                                   pattern=[[1, P]], channel_multiplier=-1).then_inc(c_const, 1)
                pool.memset(ones_bf[:], 1.0).then_inc(c_const, 1)
                pool.memset(eps_c[:], EPS).then_inc(c_const, 1)
                pool.memset(pow_c[:], -0.5).then_inc(c_const, 1)
                pool.memset(minus_c[:], -1.0).then_inc(c_const, 1)
                pool.iota(col_iota[:], pattern=[[1, P]], base=0, channel_multiplier=0,
                          allow_small_or_imprecise_dtypes=True).then_inc(c_const, 1)
                pool.iota(quarter_iota[:], pattern=[[1, CT]], base=0, channel_multiplier=0,
                          allow_small_or_imprecise_dtypes=True).then_inc(c_const, 1)
                pool.iota(part_iota[:], pattern=[[0, 1]], base=0, channel_multiplier=1,
                          allow_small_or_imprecise_dtypes=True).then_inc(c_const, 1)
                pool.iota(tile_iota[:], pattern=[[NT, B], [0, E], [1, NT]], base=0, channel_multiplier=0,
                          allow_small_or_imprecise_dtypes=True).then_inc(c_const, 1)

            @block.tensor
            def _(pe):
                pe.wait_ge(c_ident, 1)
                pe.wait_ge(d_ctx, 16)
                for b in range(B):
                    for c in range(KC):
                        nc.tensor.transpose(ps[:, 0, (c * B + b) * J:(c * B + b + 1) * J],
                                            ctx_sb[:, b, c * P:(c + 1) * P], ident[0:J, 0:J])
                pe.wait_ge(d_gw, 16)
                for c in range(KD):
                    last = nc.tensor.transpose(ps[:, 1, c * E:(c + 1) * E], gw_sb[:, c * P:(c + 1) * P],
                                               ident[0:E, 0:E])
                last.then_inc(p_ctxT, 1)
                pe.wait_ge(e_ctxT, 1)
                for w, arrived, bank in ((wk_sb, d_wk, 2), (wv_sb, d_wv, 4)):
                    pe.wait_ge(arrived, 16)
                    for t in range(KD):
                        for c in range(KC):
                            last = nc.tensor.matmul(ps[:, bank + t // 2, (t % 2) * B * J:(t % 2 + 1) * B * J],
                                                    w[:, c, t * P:(t + 1) * P],
                                                    ctxT[:, c, :, :].rearrange("p b j -> p (b j)"),
                                                    start=(c == 0), stop=(c == KC - 1))
                    last.then_inc(p_kv, 1)
                pe.wait_ge(d_wq, 16)
                for t in range(KD):
                    bank = (0, 1, 6, 7)[t]
                    for dk in range(KD):
                        last = nc.tensor.transpose(ps[:, bank, dk * P:(dk + 1) * P],
                                                   wq_sb[:, dk, t * P:(t + 1) * P], ident[:])
                last.then_inc(p_wqT, 1)
                pe.wait_ge(e_wqT, 1)
                pe.wait_ge(e_kv, 2)
                pe.wait_ge(d_wo, 16)
                for n, (kind, b, c) in enumerate(folds):
                    if n >= 4:
                        pe.wait_ge(e_lo, n - 3)
                    if kind == "A":
                        for t in range(KD):
                            last = nc.tensor.matmul(ps[:, 2 * (n % 4) + t // 2, (t % 2) * PAIR:(t % 2 + 1) * PAIR],
                                                    wqT[:, t, c * P:(c + 1) * P], kx[:, b, t, :],
                                                    start=True, stop=True)
                    else:
                        lo, hi = c * P, (c + 1) * P
                        ts = [t for t in range(KD) if t * PAIR < hi and (t + 1) * PAIR > lo]
                        for t in ts:
                            last = nc.tensor.matmul(ps[:, 2 * (n % 4), :], vx[:, b, t, lo:hi], wo_sb[:, t, :],
                                                    start=(t == ts[0]), stop=(t == ts[-1]))
                    last.then_inc(p_fold, 1)

            @block.scalar
            def _(act):
                for n in range(len(folds)):
                    act.wait_ge(p_fold, n + 1)
                    src, hi, _ = fold_bufs(n)
                    nc.scalar.activation(hi, src, ACT.Copy).then_inc(e_hi, 1)

            @block.vector
            def _(dve):
                nc.vector.memset(kx[:], 0.0)
                nc.vector.memset(vx[:], 0.0)
                dve.wait_ge(p_ctxT, 1)
                nc.vector.tensor_copy(gwT[:].rearrange("p c e -> p (c e)"), ps[:, 1, 0:KD * E])
                nc.vector.tensor_copy(ctxT[:].rearrange("p c b j -> p (c b j)"),
                                      ps[:, 0, 0:KC * B * J]).then_inc(e_ctxT, 1)
                dve.wait_ge(e_ctxT, 1)
                for m, (dst, step, bank) in enumerate(((kx, 0, 2), (vx, PAIR, 4))):
                    dve.wait_ge(p_kv, m + 1)
                    for t in range(KD):
                        for h in range(2):
                            at = step * t + h * J
                            last = nc.vector.tensor_copy(
                                dst[h * HD:(h + 1) * HD, :, t, at:at + J],
                                ps[h * HD:(h + 1) * HD, bank + t // 2,
                                   (t % 2) * B * J:(t % 2 + 1) * B * J].rearrange("p (b j) -> p b j", b=B))
                    last.then_inc(e_kv, 1)
                dve.wait_ge(p_wqT, 1)
                for t in range(KD):
                    last = nc.vector.tensor_copy(wqT[:, t, :], ps[:, (0, 1, 6, 7)[t], :])
                last.then_inc(e_wqT, 1)
                for n in range(len(folds)):
                    dve.wait_ge(e_hi, n + 1)
                    src, hi, lo = fold_bufs(n)
                    nc.vector.tensor_tensor(lo, src, hi.bitcast(F32), ALU.subtract).then_inc(e_lo, 1)
        init.close()

        tiles = ExitStack()
        XR = sb(tiles, "XR", [P, 2, TPB, D])
        XN = sb(tiles, "XN", [P, TPB, D])
        xTh = sb(tiles, "xTh", [P, TPB, D], F32R)
        xTl = sb(tiles, "xTl", [P, TPB, D], F32R)
        PR = sb(tiles, "PR", [P, TPB, H, J])
        pTh = sb(tiles, "pTh", [P, TPB, NCH, P], F32R)
        pTl = sb(tiles, "pTl", [P, TPB, NCH, P], F32R)
        X1 = sb(tiles, "X1", [P, 2, TPB, D])
        XN2 = sb(tiles, "XN2", [P, 2, TPB, D])
        xn2T = sb(tiles, "xn2T", [P, TPB, D])
        st1 = sb(tiles, "st1", [P, TPB, 6])
        mv1 = sb(tiles, "mv1", [P, TPB, 2])
        rs1 = sb(tiles, "rs1", [P, TPB])
        ve1 = sb(tiles, "ve1", [P, TPB])
        st2 = sb(tiles, "st2", [P, TPB, 6])
        mv2 = sb(tiles, "mv2", [P, TPB, 2])
        rs2 = sb(tiles, "rs2", [P, TPB])
        ve2 = sb(tiles, "ve2", [P, TPB])
        nb1 = sb(tiles, "nb1", [P, TPB])
        nb2 = sb(tiles, "nb2", [P, TPB])
        nmax = sb(tiles, "nmax", [P, TPB, H])
        smax = sb(tiles, "smax", [P, TPB, H])
        ssum = sb(tiles, "ssum", [P, TPB * H])
        srec = sb(tiles, "srec", [P, TPB * H])
        gmax = sb(tiles, "gmax", [P, TPB])
        gexp = sb(tiles, "gexp", [P, TPB, E])
        gsub = sb(tiles, "gsub", [P, TPB, E])
        gsum = sb(tiles, "gsum", [P, TPB])
        grec = sb(tiles, "grec", [P, TPB])

        d_x = [sem(f"d_x{i}") for i in range(2)]
        d_xr = [sem(f"d_xr{i}") for i in range(2)]
        d_x1 = [sem(f"d_x1{i}") for i in range(2)]
        d_xn2 = [sem(f"d_xn2{i}") for i in range(2)]
        (v_st1, v_mv1, g_ve1, g_rs1, g_nb1, a_xn, p_xT, a_xTh, v_xTl, p_s, v_max, v_nmax, a_exp, v_rec, g_prob,
         p_pT, a_tails, v_tails, a_pTh, v_pTl, p_o, g_xr, v_x1, v_st2, v_mv2, g_ve2, g_rs2, g_nb2, a_xn2, p_xn2T,
         a_xn2T, p_g, v_gmax, v_gsub, a_gexp, v_gsum, v_grec, v_gate) = (sem(n) for n in (
             "v_st1 v_mv1 g_ve1 g_rs1 g_nb1 a_xn p_xT a_xTh v_xTl p_s v_max v_nmax a_exp v_rec g_prob "
             "p_pT a_tails v_tails a_pTh v_pTl p_o g_xr v_x1 v_st2 v_mv2 g_ve2 g_rs2 g_nb2 a_xn2 p_xn2T a_xn2T p_g "
             "v_gmax v_gsub a_gexp v_gsum v_grec v_gate").split())

        FIRST, LAST = -2, NBLK
        LOOP = (4, NBLK // B + 2)

        def steps(eng, body):
            for i in range(FIRST, LOOP[0]):
                body(i, i % 2, i // 2, lambda n: 0 <= n < NBLK)
            with eng.Fori(LOOP[0] // 2, LOOP[1] // 2, 1) as k:
                for u in range(2):
                    body(2 * k + u, u, k, lambda n: True)
            for i in range(LOOP[1], LAST + 1):
                body(i, i % 2, i // 2, lambda n: 0 <= n < NBLK)

        def tile_scores(t):
            return ps[:, 2 * t:2 * t + 2, 0:HALF].rearrange("p s (h j) -> p s h j", j=J)

        TAIL = CH[-1][1]
        tails = ps[0:TAIL, 1:3, HALF:HALF + P]
        gate_sc = ps[:, 3, HALF:HALF + TPB * E].rearrange("p (t e) -> p t e", e=E)
        gate_sc7 = ps[:, 7, 0:TPB * E].rearrange("p (t e) -> p t e", e=E)

        (s_init, s_bits, s_cand, s_hit, s_cnt, s_tot, s_kept, s_best, s_thr, s_link, s_mask, s_before, s_placed, s_vals, h_hot,
         h_used, h_found, h_fsum, h_idx) = (sem(n) for n in (
             "s_init s_bits s_cand s_hit s_cnt s_tot s_kept s_best s_thr s_link s_mask s_before s_placed s_vals h_hot "
             "h_used h_found h_fsum h_idx").split())
        SLOTS = 3
        GATED = NBLK // B + 2
        CHOICE = GATED + ROUNDS // SLOTS

        def at(i, n):
            return isinstance(i, int) and i == n

        def round_at(i, slot):
            if not isinstance(i, int):
                return None
            k = (i - GATED) * SLOTS + slot - (SLOTS - 1)
            return k if 0 <= k < ROUNDS else None

        def choice(bank):
            inside, sums = ps[:, bank, 128:128 + E * NT], ps[:, bank, 256:256 + E * NT]
            return inside, sums, ps[:, bank, 384:384 + E * CAND], ps[:, bank, 416:416 + NV * CT]

        BANK = (0, 7)

        def round_bank(b, k):
            return BANK[1] if b == 1 else 0 if k % SLOTS == 0 else 3

        chained = [0]

        def link(ins):
            chained[0] += 1
            ins.then_inc(s_link, 1)
            nc.vector.wait_ge(s_link, chained[0])

        def u32(t):
            return t[:].bitcast(U32)

        def spread(t):
            return t[:].unsqueeze(2).broadcast_to([P, E, NT])

        def each_cand(t):
            return t.unsqueeze(2).broadcast_to([P, E, CAND])

        def dve_narrow(dve, b, k):
            n = b * ROUNDS + k + 1
            counts = choice(round_bank(b, k))[2].rearrange("p (e m) -> p e m", m=CAND)
            dve.wait_ge(s_tot, n)
            nc.vector.scalar_tensor_tensor(out=kept[:], in0=counts, scalar=float(CAP), in1=cand[:],
                                           op0=ALU.is_ge, op1=ALU.mult).then_inc(s_kept, 1)
            dve.wait_ge(s_kept, n)
            nc.vector.tensor_reduce(best[:], kept[:], AX.X, ALU.max).then_inc(s_best, 1)
            dve.wait_ge(s_best, n)
            nc.vector.tensor_tensor(thr[:], thr[:], best[:], ALU.max).then_inc(s_thr, 1)

        def dve_round(dve, b, k):
            n = b * ROUNDS + k + 1
            if k == 0:
                dve.wait_ge(v_gate, (b + 1) * (NBLK // B))
                if b == 0:
                    nc.vector.memset(chain[:], 1.0)
                    link(nc.vector.memset(hit[:, 0, 0, 0:1], 0.0))
                    nc.vector.memset(chain[:, :, 0:1], 0.0)
                for m in range(CAND):
                    nc.vector.memset(bits[:, :, m:m + 1], 2.0 ** (32 * m - 95))
                nc.vector.memset(thr[:], 0.0).then_inc(s_init, 1)
                dve.wait_ge(s_init, b + 1)
            else:
                dve_narrow(dve, b, k - 1)
                dve.wait_ge(s_thr, n - 1)
                dve.wait_ge(s_bits, n - 1)
            nc.vector.tensor_tensor(u32(cand), each_cand(u32(thr)), u32(bits), ALU.bitwise_or).then_inc(s_cand, 1)
            dve.wait_ge(s_cand, n)
            shape = [P, E, CAND, NT]
            nc.vector.tensor_tensor(hit[:], probs[:, b].unsqueeze(2).broadcast_to(shape),
                                    cand[:].unsqueeze(3).broadcast_to(shape), ALU.is_ge).then_inc(s_hit, 1)
            nc.vector.tensor_scalar(u32(bits), u32(bits), 2, None, ALU.logical_shift_right).then_inc(s_bits, 1)
            dve.wait_ge(s_hit, n)
            with nc.allow_low_precision(reason="counts up to 16 are exact in bfloat16"):
                nc.vector.tensor_reduce(cnt[:], hit[:].rearrange("p e m t -> p (e m) t"), AX.X,
                                        ALU.add).then_inc(s_cnt, 1)

        def pe_round(pe, b, k):
            pe.wait_ge(s_cnt, b * ROUNDS + k + 1)
            nc.tensor.matmul(choice(round_bank(b, k))[2], ones_bf[:], cnt[:], start=True, stop=True).then_inc(s_tot, 1)

        def dve_masks(dve, b):
            dve_narrow(dve, b, ROUNDS - 1)
            dve.wait_ge(s_thr, (b + 1) * ROUNDS)
            nc.vector.tensor_tensor(tied[:], probs[:, b], spread(thr), ALU.is_equal)
            link(nc.vector.tensor_tensor(above[:], probs[:, b], spread(thr), ALU.is_gt))
            with nc.allow_low_precision(reason="counts up to 16 are exact in bfloat16"):
                nc.vector.tensor_reduce(cnt[:, 0:E], above[:], AX.X, ALU.add).then_inc(s_mask, 1)

        def pe_before(pe, b, m):
            pe.wait_ge(s_mask, 2 * b + m + 1)
            inside, sums, counts, _ = choice(BANK[b])
            if m == 0:
                nc.tensor.matmul(counts[:, 0:E], ones_bf[:], cnt[:, 0:E], start=True, stop=True)
            flat = (tied, chosen)[m][:].rearrange("p c t -> p (c t)")
            nc.tensor.matmul(inside, before_bf[:], flat, start=True, stop=True)
            nc.tensor.matmul(sums, ones_bf[:], flat, start=True, stop=True).then_inc(s_before, 1)

        def dve_places(dve, b, m):
            dve.wait_ge(s_before, 2 * b + m + 1)
            inside, sums, _, _ = choice(BANK[b])
            link(nc.vector.tensor_tensor_scan(run[:].rearrange("p c t -> p (c t)"),
                                              chain[:].rearrange("p c t -> p (c t)"), sums, 0.0, ALU.mult, ALU.add))
            link(nc.vector.tensor_tensor(run2[:], run[:], sums.rearrange("p (c t) -> p c t", t=NT), ALU.subtract))
            nc.vector.tensor_tensor(place[:], run2[:], inside.rearrange("p (c t) -> p c t", t=NT),
                                    ALU.add).then_inc(s_placed, 1)
            dve.wait_ge(s_placed, 2 * b + m + 1)

        def dve_chosen(dve, b):
            dve.wait_ge(s_before, 2 * b + 1)
            nc.vector.tensor_scalar(room[:], choice(BANK[b])[2][:, 0:E], -1.0, float(CAP), ALU.mult, ALU.add)
            dve_places(dve, b, 0)
            link(nc.vector.tensor_tensor(q1[:], place[:], spread(room), ALU.is_lt))
            link(nc.vector.tensor_tensor(q2[:], q1[:], tied[:], ALU.mult))
            nc.vector.tensor_tensor(chosen[:], q2[:], above[:], ALU.add).then_inc(s_mask, 1)

        def dve_gate_parts(b):
            prob = probs[:, b]
            link(nc.vector.tensor_copy(gp[0][:], prob))
            link(nc.vector.tensor_tensor(rest1[:], prob, gp[0][:], ALU.subtract))
            link(nc.vector.tensor_copy(gp[1][:], rest1[:]))
            link(nc.vector.tensor_tensor(rest2[:], rest1[:], gp[1][:], ALU.subtract))
            link(nc.vector.tensor_copy(gp[2][:], rest2[:]))

        def dve_rows(dve, b):
            link(nc.vector.tensor_scalar(q1[:], place[:], float(P), None, ALU.is_ge))
            link(nc.vector.scalar_tensor_tensor(out=q2[:], in0=place[:], scalar=float(2 * P), in1=q1[:],
                                                op0=ALU.is_ge, op1=ALU.add))
            link(nc.vector.scalar_tensor_tensor(out=quarter[:], in0=place[:], scalar=float(3 * P), in1=q2[:],
                                                op0=ALU.is_ge, op1=ALU.add))
            link(nc.vector.scalar_tensor_tensor(out=q1[:], in0=quarter[:], scalar=float(-P), in1=place[:],
                                                op0=ALU.mult, op1=ALU.add))
            link(nc.vector.scalar_tensor_tensor(out=q2[:], in0=q1[:], scalar=1.0, in1=chosen[:],
                                                op0=ALU.add, op1=ALU.mult))
            link(nc.vector.tensor_scalar(row[:, b], q2[:], -1.0, None, ALU.add))

        def dve_vals(b):
            shape = [P, E * NT, CT]

            def each(t):
                return t.unsqueeze(2).broadcast_to(shape)

            link(nc.vector.tensor_tensor(inq[:].rearrange("p c t q -> p (c t) q"),
                                         each(quarter[:].rearrange("p c t -> p (c t)")),
                                         quarter_iota[:].unsqueeze(1).broadcast_to(shape), ALU.is_equal))
            numbers = [part_iota[:].broadcast_to([P, E * NT]), tile_iota[:, b].rearrange("p e t -> p (e t)"),
                       *(g[:].rearrange("p c t -> p (c t)") for g in gp)]
            for v, number in enumerate(numbers):
                last = nc.vector.tensor_tensor(vals[:, b, :, :, v, :].rearrange("p c t q -> p (c t) q"),
                                               inq[:].rearrange("p c t q -> p (c t) q"), each(number), ALU.mult)
            last.then_inc(s_vals, 1)

        rows_flat = row[:].rearrange("p b c t -> p (b c t)")
        vals_flat = vals[:].rearrange("p b c t v q -> p (b c t v q)")
        flat_idx = tok_idx[:].rearrange("p c q -> p (c q)")
        flat_gate = tok_gate[:].rearrange("p c q -> p (c q)")

        def dve_one_hot(c):
            shape = [P, NT, P]
            nc.vector.tensor_tensor(hot[:], rows_flat[:, bass.ds(c * NT, NT)].unsqueeze(2).broadcast_to(shape),
                                    col_iota[:].unsqueeze(1).broadcast_to(shape), ALU.is_equal).then_inc(h_hot, 1)

        def pe_lookup(pe, c, bank):
            pe.wait_ge(h_hot, c + 1)
            for t in range(NT):
                last = nc.tensor.matmul(choice(bank)[3], hot[:, t, :],
                                        vals_flat[:, bass.ds(c * (NT * NV * CT) + t * NV * CT, NV * CT)],
                                        start=(t == 0), stop=(t == NT - 1))
            last.then_inc(h_used, 1)

        def dve_found(dve, c, bank):
            dve.wait_ge(h_used, c + 1)
            nc.vector.tensor_copy(found[:].rearrange("p v q -> p (v q)"), choice(bank)[3]).then_inc(h_found, 1)
            dve.wait_ge(h_found, c + 1)
            nc.vector.tensor_tensor(fsum[:], found[:, 2, :], found[:, 3, :], ALU.add).then_inc(h_fsum, 1)
            nc.vector.scalar_tensor_tensor(out=flat_idx[:, bass.ds(c * CT, CT)], in0=found[:, 1, :], scalar=float(P),
                                           in1=found[:, 0, :], op0=ALU.mult, op1=ALU.add)
            dve.wait_ge(h_fsum, c + 1)
            nc.vector.tensor_tensor(flat_gate[:, bass.ds(c * CT, CT)], fsum[:], found[:, 4, :],
                                    ALU.add).then_inc(h_idx, 1)

        f_raw = [sem(f"f_raw{i}") for i in range(2)]
        f_hh = sem("f_hh")
        f_passed = sem("f_passed")
        (f_w1h, f_w2h, f_w1l, f_w2l, f_up, f_gelu, f_h, f_down, f_gidx, f_sidx, f_tr, f_eTh, f_eTl, f_ya, f_yd,
         f_yfree) = (sem(f"f_{n}") for n in
                     "w1h w2h w1l w2l up gelu h down gidx sidx tr eTh eTl ya yd yfree".split())
        f_rows = sem("f_rows")
        f_scat = sem("f_scat")
        w1_g = w1.rearrange("e (k p) f -> e p k f", p=P)
        w2_g = w2.rearrange("e (k p) d -> e p k d", p=P)

        def passed(eng, sem, value):
            eng.wait_ge(sem, value)
            eng.sem_inc(f_passed, 1)

        def sp_weights(sp, i, e, g, wait):
            a, b = w1_g[e, :, :, g * GF * P:(g + 1) * GF * P], w2_g[e, :, g * GF:(g + 1) * GF, :]
            if wait:
                passed(sp, f_w2l, i * KF + (g - 1) * GF)
            sp.dma_start(w1_raw[:, g % 2], a).then_inc(f_raw[g % 2], 16)
            sp.dma_start(w2_raw[:, g % 2], b).then_inc(f_raw[g % 2], 16)

        def sp_attention(sp):
            def step(i, u, half, has):
                lanes = []
                if has_(has, i + 4):
                    lanes.append(("x", i + 4))
                if has_(has, i - 2):
                    lanes.append(("out", i - 2))
                if has_(has, i + 1):
                    lanes.append(("xr", i + 1))
                for kind, n in lanes:
                    if kind == "x":
                        src = x_blk[n]
                        free = sp.snap(n - 1)
                        if early(i, n, 2):
                            sp.wait_ge(a_xn, free)
                        sp.dma_start(XB[:, u], src).then_inc(d_x[u], 16)
                    elif kind == "xr":
                        src = x_blk[n]
                        free = sp.snap(n - 1)
                        if early(i, n, 2):
                            sp.wait_ge(v_x1, free)
                        sp.dma_start(XR[:, 1 - u], src).then_inc(d_xr[1 - u], 16)
                    else:
                        to1, to2, done = out_blk[n], xn2_blk[n], sp.snap(n + 1)
                        sp.wait_ge(v_x1, done)
                        sp.dma_start(to1, X1[:, u]).then_inc(d_x1[u], 16)
                        sp.wait_ge(a_xn2, done)
                        sp.dma_start(to2, XN2[:, u]).then_inc(d_xn2[u], 16)

            def has_(has, n):
                return has(n) if isinstance(n, int) else True

            def early(i, n, k):
                return n >= k if isinstance(n, int) else True

            for n in range(2):
                sp.dma_start(XB[:, n], x_blk[n]).then_inc(d_x[n], 16)
            for i in range(FIRST, 4):
                step(i, i % 2, i // 2, lambda n: 0 <= n < NBLK)
            with sp.Fori(2, NBLK // 2 - 2, 1) as k:
                for u in range(2):
                    step(2 * k + u, u, k, lambda n: True)
            for i in range(NBLK - 4, LAST + 1):
                step(i, i % 2, i // 2, lambda n: 0 <= n < NBLK)
                if i == NBLK - 4:
                    for g in range(2):
                        sp_weights(sp, 0, 0, g, False)
            step(LAST + 1, (LAST + 1) % 2, (LAST + 1) // 2, lambda n: 0 <= n < NBLK)

        def pool_rstd(pool, mv, ve, rs, nb, ready, mid, scaled, done, used, n):
            pool.wait_ge(ready, n + 1)
            if not isinstance(n, int) or n > 0:
                pool.wait_ge(used, n)
            pool.tensor_tensor(nb[:], mv[:, :, 0], minus_c[:], ALU.mult)
            pool.tensor_tensor(ve[:], mv[:, :, 1], eps_c[:], ALU.add).then_inc(mid, 1)
            pool.wait_ge(mid, n + 1)
            pool.tensor_tensor(rs[:], ve[:], pow_c[:], ALU.pow).then_inc(scaled, 1)
            pool.wait_ge(scaled, n + 1)
            pool.tensor_tensor(nb[:], nb[:], rs[:], ALU.mult).then_inc(done, 1)

        def pool_attention(pool):
            def step(i, u, half, has):
                if has(i - 1):
                    pool.wait_ge(d_xr[1 - u], 16 * half + 16 * u)
                    pool.tensor_tensor(XR[:, 1 - u], XR[:, 1 - u], bo_rows[:], ALU.add).then_inc(g_xr, 1)
                if has(i - 2):
                    pool_rstd(pool, mv2, ve2, rs2, nb2, v_mv2, g_ve2, g_rs2, g_nb2, a_xn2, i - 2)
                if has(i + 2):
                    pool_rstd(pool, mv1, ve1, rs1, nb1, v_mv1, g_ve1, g_rs1, g_nb1, a_xn, i + 2)
                if has(i):
                    for t in range(TPB):
                        pool.wait_ge(v_rec, 2 * i + t + 1)
                        over = srec[:, t * H:(t + 1) * H].unsqueeze(2).broadcast_to([P, H, J])
                        pool.tensor_tensor(PR[:, t], PR[:, t], over, ALU.mult).then_inc(g_prob, 1)
            steps(pool, step)

        def act_gate_exp(act, n):
            act.wait_ge(v_gsub, n + 1)
            nc.scalar.activation(gexp[:], gsub[:], ACT.Exp).then_inc(a_gexp, 1)

        def act_xn2T(act, n):
            act.wait_ge(p_xn2T, n + 1)
            nc.scalar.activation(xn2T[:], ps[:, 6:8, :], ACT.Copy).then_inc(a_xn2T, 1)

        def act_normalise(act, src, rs, nb, dst, ready, done, n):
            act.wait_ge(ready, n + 1)
            for t in range(TPB):
                last = nc.scalar.activation(dst[:, t, :], src[:, t, :], ACT.Identity, bias=nb[:, t:t + 1],
                                            scale=rs[:, t:t + 1])
            last.then_inc(done, 1)

        def act_attention(act):
            def exp(i, t):
                act.wait_ge(v_nmax, 2 * i + t + 1)
                for h in range(H):
                    last = nc.scalar.activation(PR[:, t, h, :], tile_scores(t)[:, h // 4, h % 4, :], ACT.Exp,
                                                bias=nmax[:, t, h:h + 1], scale=HD ** -0.5,
                                                accum_out=ssum[:, t * H + h:t * H + h + 1])
                last.then_inc(a_exp, 1)

            def step(i, u, half, has):
                if has(i - 1):
                    act.wait_ge(p_pT, i)
                    nc.scalar.activation(pTh[0:TAIL, :, NCH - 1, :], tails, ACT.Copy).then_inc(a_tails, 1)
                    nc.scalar.activation(pTh[:, :, 0:NCH - 1, :],
                                         ps[:, 6:8, :].rearrange("p t (c q) -> p t c q", q=P),
                                         ACT.Copy).then_inc(a_pTh, 1)
                if has(i - 3):
                    act_gate_exp(act, i - 3)
                if has(i):
                    exp(i, 0)
                if has(i + 1):
                    act.wait_ge(p_xT, i + 2)
                    nc.scalar.activation(xTh[:], ps[:, 6:8, :], ACT.Copy).then_inc(a_xTh, 1)
                if has(i - 2):
                    if not isinstance(i, int) or i >= 4:
                        act.wait_ge(d_xn2[u], 16 * half - 16)
                    act_normalise(act, X1[:, u], rs2, nb2, XN2[:, u], g_nb2, a_xn2, i - 2)
                if has(i):
                    exp(i, 1)
                if has(i + 2):
                    act_normalise(act, XB[:, u], rs1, nb1, XN, g_nb1, a_xn, i + 2)
                if has(i - 2):
                    act_xn2T(act, i - 2)
            steps(act, step)

        def stats(src, st, done):
            for t in range(TPB):
                last = nc.vector.bn_stats(st[:, t, :], src[:, t, :])
            last.then_inc(done, 1)

        def aggregate(st, mv, done):
            for t in range(TPB):
                last = nc.vector.bn_aggr(mv[:, t, :], st[:, t, :])
            last.then_inc(done, 1)

        def dve_gate_scores(dve, n, scores):
            dve.wait_ge(p_g, n + 1)
            nc.vector.tensor_reduce(gmax[:], scores, AX.X, ALU.max).then_inc(v_gmax, 1)
            dve.wait_ge(v_gmax, n + 1)
            nc.vector.tensor_tensor(gsub[:], scores, gmax[:].unsqueeze(2).broadcast_to([P, TPB, E]),
                                    ALU.subtract).then_inc(v_gsub, 1)

        def dve_gate(dve, n):
            dve.wait_ge(a_gexp, n + 1)
            nc.vector.tensor_reduce(gsum[:], gexp[:], AX.X, ALU.add).then_inc(v_gsum, 1)
            dve.wait_ge(v_gsum, n + 1)
            nc.vector.reciprocal(grec[:], gsum[:]).then_inc(v_grec, 1)
            dve.wait_ge(v_grec, n + 1)
            b, pair = n // (NBLK // B), n % (NBLK // B) if isinstance(n, int) else n & (NBLK // B - 1)
            flat = probs[:].rearrange("p b e t -> p (b e t)")
            for t in range(TPB):
                to = b * (E * NT) + pair * TPB + t
                last = nc.vector.tensor_scalar(flat[:, bass.ds(to, E, step=NT)], gexp[:, t, :],
                                               grec[:, t:t + 1], None, ALU.mult)
            last.then_inc(v_gate, 1)

        def dve_x1(dve, n, u, stored):
            dve.wait_ge(p_o, n + 1)
            dve.wait_ge(g_xr, n + 1)
            if stored is not None:
                dve.wait_ge(d_x1[u], stored)
            nc.vector.tensor_tensor(X1[:, u], ps[:, 4:6, :], XR[:, u], ALU.add).then_inc(v_x1, 1)

        def dve_attention(dve):
            def maximum(i, t):
                dve.wait_ge(p_s, 2 * i + t + 1)
                nc.vector.tensor_reduce(smax[:, t, :].rearrange("p (s h) -> p s h", s=2), tile_scores(t),
                                        AX.X, ALU.max).then_inc(v_max, 1)
                dve.wait_ge(v_max, 2 * i + t + 1)
                nc.vector.tensor_scalar(nmax[:, t, :], smax[:, t, :], -HD ** -0.5, None,
                                        ALU.mult).then_inc(v_nmax, 1)

            def step(i, u, half, has):
                if round_at(i, 0) is not None:
                    dve_round(dve, 0, round_at(i, 0))
                if at(i, CHOICE + 1):
                    dve_chosen(dve, 0)
                if has(i - 1):
                    dve.wait_ge(a_tails, i)
                    nc.vector.tensor_tensor(pTl[0:TAIL, :, NCH - 1, :], tails,
                                            pTh[0:TAIL, :, NCH - 1, :].bitcast(F32),
                                            ALU.subtract).then_inc(v_tails, 1)
                    dve.wait_ge(a_pTh, i)
                    nc.vector.tensor_tensor(pTl[:, :, 0:NCH - 1, :],
                                            ps[:, 6:8, :].rearrange("p t (c q) -> p t c q", q=P),
                                            pTh[:, :, 0:NCH - 1, :].bitcast(F32), ALU.subtract).then_inc(v_pTl, 1)
                if round_at(i, 1) is not None:
                    dve_round(dve, 0, round_at(i, 1))
                if has(i - 3):
                    dve_gate_scores(dve, i - 3, gate_sc)
                if has(i - 2):
                    dve_x1(dve, i - 2, u, 16 * half - 16 if not isinstance(i, int) or i >= 4 else None)
                if at(i, CHOICE + 1):
                    dve_places(dve, 0, 1)
                    dve_rows(dve, 0)
                    dve_vals(0)
                    dve_one_hot(0)
                if has(i):
                    maximum(i, 0)
                if has(i - 2):
                    dve.wait_ge(v_x1, i - 1)
                    stats(X1[:, u], st2, v_st2)
                if has(i + 2):
                    dve.wait_ge(d_x[u], 16 * half + 32)
                    if has(i + 1):
                        dve.wait_ge(g_nb1, i + 2)
                    if has(i - 2):
                        dve.wait_ge(v_st2, i - 1)
                    stats(XB[:, u], st1, v_st1)
                elif has(i - 2):
                    dve.wait_ge(v_st2, i - 1)
                if has(i - 2):
                    aggregate(st2, mv2, v_mv2)
                if at(i, CHOICE + 1):
                    dve_found(dve, 0, BANK[0])
                if has(i + 2):
                    dve.wait_ge(v_st1, i + 3)
                if has(i):
                    maximum(i, 1)
                if has(i + 2):
                    aggregate(st1, mv1, v_mv1)
                if has(i - 3):
                    dve_gate(dve, i - 3)
                if has(i + 1):
                    dve.wait_ge(a_xTh, i + 2)
                    nc.vector.tensor_tensor(xTl[:], ps[:, 6:8, :], xTh[:].bitcast(F32),
                                            ALU.subtract).then_inc(v_xTl, 1)
                if has(i):
                    for t in range(TPB):
                        dve.wait_ge(a_exp, 2 * i + t + 1)
                        nc.vector.reciprocal(srec[:, t * H:(t + 1) * H],
                                             ssum[:, t * H:(t + 1) * H]).then_inc(v_rec, 1)
                if round_at(i, 2) is not None:
                    dve_round(dve, 0, round_at(i, 2))
                if at(i, GATED + 1):
                    dve_gate_parts(0)
                if at(i, CHOICE):
                    dve_masks(dve, 0)
            steps(dve, step)
            dve_x1(dve, NBLK - 1, (NBLK - 1) % 2, 16 * (NBLK // 2 - 1))
            dve.wait_ge(v_x1, NBLK)
            stats(X1[:, (NBLK - 1) % 2], st2, v_st2)
            dve.wait_ge(g_nb2, NBLK - 1)
            dve.wait_ge(v_st2, NBLK)
            aggregate(st2, mv2, v_mv2)

        def pe_gate(scores):
            for t in range(TPB):
                for dk in range(KD):
                    last = nc.tensor.matmul(scores[:, t, :], xn2T[:, t, dk * P:(dk + 1) * P], gwT[:, dk, :],
                                            start=(dk == 0), stop=(dk == KD - 1))
            last.then_inc(p_g, 1)

        def pe_xn2T(u):
            for t in range(TPB):
                for dk in range(KD):
                    last = nc.tensor.transpose(ps[:, 6 + t, dk * P:(dk + 1) * P],
                                               XN2[:, u, t, dk * P:(dk + 1) * P], ident[:])
            last.then_inc(p_xn2T, 1)

        def pe_attention(pe):
            def three(psum, pairs, **kw):
                n = len(pairs)
                for k, (wh, wl, mh, ml) in enumerate(pairs):
                    nc.tensor.matmul(psum, wh, mh, start=(k == 0), stop=False, **kw)
                    nc.tensor.matmul(psum, wh, ml, start=False, stop=False, **kw)
                    last = nc.tensor.matmul(psum, wl, mh, start=False, stop=(k == n - 1), **kw)
                return last

            def second_norm(i, u, has):
                pe.wait_ge(a_xn2, i - 1)
                if has(i + 1):
                    pe.wait_ge(v_xTl, i + 2)
                pe_xn2T(u)

            def step(i, u, half, has):
                if round_at(i - 1, 2) is not None:
                    pe_round(pe, 0, round_at(i - 1, 2))
                if at(i, CHOICE + 1):
                    pe_before(pe, 0, 0)
                if has(i - 1):
                    pe.wait_ge(g_prob, 2 * i - 1)
                    if has(i - 3):
                        pe.wait_ge(a_xn2T, i - 2)
                    elif has(i):
                        pe.wait_ge(v_xTl, i + 1)
                    flat = PR[:].rearrange("p t h j -> p (t h j)")
                    for t in range(TPB):
                        if t:
                            pe.wait_ge(g_prob, 2 * i)
                        for c, (c0, n) in enumerate(CH):
                            dst = tails[:, t, :] if c == NCH - 1 else ps[:, 6 + t, c0:c0 + P]
                            last = nc.tensor.transpose(dst, flat[:, t * HJ + c0:t * HJ + c0 + n], ident[:])
                    last.then_inc(p_pT, 1)
                if has(i - 3):
                    pe.wait_ge(a_xn2T, i - 2)
                    pe_gate(gate_sc)
                if round_at(i, 0) is not None:
                    pe_round(pe, 0, round_at(i, 0))
                if at(i, CHOICE + 1):
                    pe_before(pe, 0, 1)
                if has(i):
                    pe.wait_ge(v_xTl, i + 1)
                    if isinstance(i, int):
                        batch = i // (NBLK // B)
                        base = [batch * KD * HJ + dk * HJ for dk in range(KD)]
                    else:
                        base0 = pe.snap(i // (NBLK // B) * (KD * HJ))
                        base = [base0 + dk * HJ for dk in range(KD)]
                    fh, fl = (m[:].rearrange("p b k n -> p (b k n)") for m in (AH, AL))
                    for t in range(TPB):
                        for part in range(2):
                            if has(i - 1) and (t, part) == (0, 1):
                                pe.wait_ge(v_tails, i)
                            if has(i - 3) and (t, part) == (1, 1):
                                pe.wait_ge(v_gsub, i - 2)
                            if round_at(i, 1) is not None and (t, part) == (1, 1):
                                pe_round(pe, 0, round_at(i, 1))
                            last = three(ps[:, 2 * t + part, 0:HALF],
                                         [(xTh[:, t, dk * P:(dk + 1) * P], xTl[:, t, dk * P:(dk + 1) * P],
                                           fh[:, bass.ds(base[dk] + part * HALF, HALF)],
                                           fl[:, bass.ds(base[dk] + part * HALF, HALF)])
                                          for dk in range(KD)])
                        last.then_inc(p_s, 1)
                if has(i + 1):
                    pe.wait_ge(a_xn, i + 2)
                    if has(i - 1):
                        pe.wait_ge(v_pTl, i)
                    for t in range(TPB):
                        for dk in range(KD):
                            last = nc.tensor.transpose(ps[:, 6 + t, dk * P:(dk + 1) * P],
                                                       XN[:, t, dk * P:(dk + 1) * P], ident[:])
                    last.then_inc(p_xT, 1)
                if has(i - 1):
                    pe.wait_ge(v_pTl, i)
                    if has(i - 2):
                        pe.wait_ge(v_x1, i - 1)
                    n = i - 1
                    if isinstance(n, int):
                        batch = n // (NBLK // B)
                        base = [(batch * NCH + c) * D for c in range(NCH)]
                    else:
                        base0 = pe.snap(n // (NBLK // B) * (NCH * D))
                        base = [base0 + c * D for c in range(NCH)]
                    fh, fl = (m[:].rearrange("p b k n -> p (b k n)") for m in (BH, BL))
                    for t in range(TPB):
                        last = three(ps[:, 4 + t, :],
                                     [(pTh[0:k, t, c, :], pTl[0:k, t, c, :],
                                       fh[0:k, bass.ds(base[c], D)], fl[0:k, bass.ds(base[c], D)])
                                      for c, (_, k) in enumerate(CH)])
                        if t == 0 and has(i - 2) and not at(i, NBLK):
                            second_norm(i, u, has)
                    last.then_inc(p_o, 1)
                elif has(i - 2):
                    second_norm(i, u, has)
                if at(i, CHOICE + 1):
                    pe.wait_ge(s_vals, 1)
                    pe_lookup(pe, 0, BANK[0])
                    second_norm(i, u, has)
            steps(pe, step)
        tiles.close()
        attn.close()

        ffn = ExitStack()
        SLOTS1, SLOTS2 = 4, 8
        w1h = sb(ffn, "w1h", [P, SLOTS1, KD, P], F32R)
        w1l = sb(ffn, "w1l", [P, SLOTS1, KD, P], F32R)
        w2h = sb(ffn, "w2h", [P, SLOTS2, D], F32R)
        w2l = sb(ffn, "w2l", [P, SLOTS2, D], F32R)
        eTh = sb(ffn, "eTh", [P, 2, KD, CAP], F32R)
        eTl = sb(ffn, "eTl", [P, 2, KD, CAP], F32R)
        hf = sb(ffn, "hf", [P, 2, CAP])
        hh = sb(ffn, "hh", [P, 4, CAP], F32R)
        hl = sb(ffn, "hl", [P, 4, CAP], F32R)
        Y = sb(ffn, "Y", [P, CT, D])

        flat_eTh = eTh[:].rearrange("p b k n -> p (b k n)")
        flat_eTl = eTl[:].rearrange("p b k n -> p (b k n)")
        EB = KD * CAP

        def columns(eng, body):
            body(0, True)
            body(1, True)
            with eng.Fori(2, COLS - 1, 1) as i:
                body(i, True)
            body(COLS - 1, False)

        ROUNDS_AT = range(2, 2 + ROUNDS)
        CHOICE_AT = ROUNDS_AT[-1] + 1
        LOOKUP = 3
        TURNS = tuple(range(KF // 2, KF, 2))

        def sp_experts(sp):
            for g in range(2, G):
                sp_weights(sp, 0, 0, g, True)
            with sp.Fori(1, COLS, 1) as i:
                for g in range(G):
                    sp_weights(sp, i, i & (E - 1), g, True)

        def pool_experts(pool):
            def gather(i, first):
                if not first:
                    passed(pool, f_rows, i * CT * 16)
                pool.wait_ge(h_idx, i + 1)
                pool.tensor_copy(gidx[:], flat_idx[:, bass.ds(i * CT, CT)]).then_inc(f_gidx, 1)
                passed(pool, f_gidx, i + 1)
                if first:
                    pool.wait_ge(a_xn, NBLK)
                    for u in range(2):
                        pool.wait_ge(d_xn2[u], 16 * NBLK // B // 2)
                else:
                    passed(pool, f_tr, i * KD)
                src = xn2_rows[0:S, :] if first else xn2_rows
                for c in range(CT):
                    pool.indirect_dma_start(out=rows_in[:, c, :], out_offset=None, in_=src,
                                            in_offset=bass.IndirectOffsetOnAxis(ap=gidx[:, c:c + 1], axis=0),
                                            ).then_inc(f_rows, 16)

            def body(i, more):
                if more:
                    gather(i + 1, False)
                pool.tensor_copy(sidx[:], flat_idx[:, bass.ds(i * CT, CT)]).then_inc(f_sidx, 1)
                passed(pool, f_sidx, i + 1)
                passed(pool, f_ya, i + 1)
                passed(pool, f_yd, i + 1)
                for c in range(CT):
                    pool.indirect_dma_start(out=out_rows,
                                            out_offset=bass.IndirectOffsetOnAxis(ap=sidx[:, c:c + 1], axis=0),
                                            in_=Y[:, c, :], in_offset=None, compute_op=ALU.add,
                                            ).then_inc(f_scat, 16)
                    passed(pool, f_scat, (i * CT + c + 1) * 16)
                pool.sem_inc(f_yfree, 1)

            gather(0, True)
            pool_rstd(pool, mv2, ve2, rs2, nb2, v_mv2, g_ve2, g_rs2, g_nb2, a_xn2, NBLK - 1)
            for u in range(2):
                pool.wait_ge(d_xn2[u], 16 * NBLK // 2)
                pool.wait_ge(d_x1[u], 16 * NBLK // 2)
            columns(pool, body)

        def act_experts(act):
            def weights(i, f, wait1, wait2):
                g, j = divmod(f, GF)
                if j == 0:
                    act.wait_ge(f_raw[g % 2], 64 * i + 32 * (g // 2 + 1))
                if wait1 is not None:
                    act.wait_ge(f_up, wait1)
                nc.scalar.activation(w1h[:, f % SLOTS1], w1_raw[:, g % 2, :, j * P:(j + 1) * P],
                                     ACT.Copy).then_inc(f_w1h, 1)
                if wait2 is not None:
                    act.wait_ge(f_down, wait2)
                nc.scalar.activation(w2h[:, f % SLOTS2], w2_raw[:, g % 2, j, :], ACT.Copy).then_inc(f_w2h, 1)

            def token_chunk(i, k, bank):
                act.wait_ge(f_tr, i * KD + k + 1)
                half = (i & 1) * EB
                nc.scalar.activation(flat_eTh[:, bass.ds(half + k * CAP, CAP)], ps[:, bank, :],
                                     ACT.Copy).then_inc(f_eTh, 1)

            def body(i, more):
                for f in range(KF):
                    if f + 2 < KF:
                        weights(i, f + 2, i * KF + f - 1 if f >= 2 else None,
                                i * KF + f - 5 if f >= 6 else None)
                    elif more:
                        weights(i + 1, f + 2 - KF, i * KF + f - 1, i * KF + f - 5)
                    act.wait_ge(f_up, i * KF + f + 1)
                    if f >= 2:
                        act.wait_ge(f_h, i * KF + f - 1)
                    nc.scalar.activation(hf[:, f % 2, :], ps[:, 4 + f % 2, :], ACT.Gelu).then_inc(f_gelu, 1)
                    if at(i, 0) and f == 0:
                        act_gate_exp(act, NBLK - 2)
                        act_xn2T(act, NBLK - 1)
                    if at(i, 0) and f == 2:
                        act_gate_exp(act, NBLK - 1)
                    if more and f - 1 in TURNS:
                        token_chunk(i + 1, TURNS.index(f - 1), 6)
                act.wait_ge(f_down, (i + 1) * KF)
                act.wait_ge(f_yfree, i + 1)
                for c in range(CT // 2, CT):
                    last = nc.scalar.activation(Y[:, c, :], ps[:, c, :], ACT.Copy,
                                                scale=flat_gate[:, bass.ds(i * CT + c, 1)])
                last.then_inc(f_ya, 1)

            act.wait_ge(p_o, NBLK)
            for f in range(2):
                weights(0, f, None, None)
            u = (NBLK - 1) % 2
            act.wait_ge(d_xn2[u], 16 * (NBLK // 2 - 1))
            act_normalise(act, X1[:, u], rs2, nb2, XN2[:, u], g_nb2, a_xn2, NBLK - 1)
            for k in range(KD):
                token_chunk(0, k, k)
            columns(act, body)

        def dve_experts(dve):
            def weights(f, n):
                g, j = divmod(f, GF)
                dve.wait_ge(f_w1h, n + 1)
                nc.vector.tensor_tensor(w1l[:, f % SLOTS1], w1_raw[:, g % 2, :, j * P:(j + 1) * P],
                                        w1h[:, f % SLOTS1].bitcast(F32), ALU.subtract).then_inc(f_w1l, 1)
                dve.wait_ge(f_w2h, n + 1)
                nc.vector.tensor_tensor(w2l[:, f % SLOTS2], w2_raw[:, g % 2, j, :],
                                        w2h[:, f % SLOTS2].bitcast(F32), ALU.subtract).then_inc(f_w2l, 1)

            def token_chunk(i, k, bank):
                dve.wait_ge(f_eTh, i * KD + k + 1)
                at = bass.ds((i & 1) * EB + k * CAP, CAP)
                nc.vector.tensor_tensor(flat_eTl[:, at], ps[:, bank, :], flat_eTh[:, at].bitcast(F32),
                                        ALU.subtract).then_inc(f_eTl, 1)

            def body(i, more):
                for f in range(KF):
                    if f + 2 < KF or more:
                        weights((f + 2) % KF, i * KF + f + 2)
                    dve.wait_ge(f_gelu, i * KF + f + 1)
                    if f >= 4:
                        dve.wait_ge(f_down, i * KF + f - 3)
                    nc.vector.tensor_copy(hh[:, f % 4], hf[:, f % 2, :]).then_inc(f_hh, 1)
                    dve.wait_ge(f_hh, i * KF + f + 1)
                    nc.vector.tensor_tensor(hl[:, f % 4], hf[:, f % 2, :], hh[:, f % 4].bitcast(F32),
                                            ALU.subtract).then_inc(f_h, 1)
                    if more and f == LOOKUP - 2:
                        dve_one_hot(i + 1)
                    if more and f == LOOKUP:
                        dve_found(dve, i + 1, BANK[1])
                    if at(i, 0) and f == 0:
                        dve_gate(dve, NBLK - 2)
                    if at(i, 0) and f == 1:
                        dve_gate_scores(dve, NBLK - 1, gate_sc7)
                    if at(i, 0) and f == 2:
                        dve_gate(dve, NBLK - 1)
                    q = i * KF + f if isinstance(i, int) else None
                    if q in ROUNDS_AT:
                        dve_round(dve, 1, q - ROUNDS_AT[0])
                    if q == CHOICE_AT:
                        dve_masks(dve, 1)
                    if q == CHOICE_AT + 2:
                        dve_chosen(dve, 1)
                    if q == CHOICE_AT + 4:
                        dve_places(dve, 1, 1)
                        dve_rows(dve, 1)
                    if q == CHOICE_AT + 5:
                        dve_gate_parts(1)
                    if q == CHOICE_AT + 6:
                        dve_vals(1)
                    if more and f - 1 in TURNS:
                        token_chunk(i + 1, TURNS.index(f - 1), 6)
                dve.wait_ge(f_down, (i + 1) * KF)
                dve.wait_ge(f_yfree, i + 1)
                for c in range(CT // 2):
                    last = nc.vector.tensor_scalar(Y[:, c, :], ps[:, c, :], flat_gate[:, bass.ds(i * CT + c, 1)],
                                                   None, ALU.mult)
                last.then_inc(f_yd, 1)

            dve.sem_inc(f_yfree, 1)
            for f in range(2):
                weights(f, f)
            dve_gate_scores(dve, NBLK - 2, gate_sc7)
            for k in range(KD):
                token_chunk(0, k, k)
            columns(dve, body)

        def pe_experts(pe):
            def transposes(i, k, bank):
                if k == 0:
                    pe.wait_ge(f_rows, 16 * CT * (i + 1))
                if bank == 6:
                    pe.wait_ge(f_eTl, i * KD + k)
                for c in range(CT):
                    last = nc.tensor.transpose(ps[:, bank, c * P:(c + 1) * P],
                                               rows_in[:, c, k * P:(k + 1) * P], ident[:])
                last.then_inc(f_tr, 1)

            def up(i, f):
                pe.wait_ge(f_w1l, i * KF + f + 1)
                if f == 0:
                    pe.wait_ge(f_eTl, (i + 1) * KD)
                if at(i, 0) and f == 0:
                    pe.wait_ge(v_x1, NBLK)
                if f >= 2:
                    pe.wait_ge(f_gelu, i * KF + f - 1)
                for k in range(KD):
                    chunk = bass.ds(halves[0] + k * CAP, CAP)
                    wh, wl = w1h[:, f % SLOTS1, k, :], w1l[:, f % SLOTS1, k, :]
                    nc.tensor.matmul(ps[:, 4 + f % 2, :], wh, flat_eTh[:, chunk], start=(k == 0), stop=False)
                    nc.tensor.matmul(ps[:, 4 + f % 2, :], wh, flat_eTl[:, chunk], start=False, stop=False)
                    last = nc.tensor.matmul(ps[:, 4 + f % 2, :], wl, flat_eTh[:, chunk], start=False,
                                            stop=(k == KD - 1))
                last.then_inc(f_up, 1)

            def down(i, f):
                pe.wait_ge(f_h, i * KF + f + 1)
                pe.wait_ge(f_w2l, i * KF + f + 1)
                for c in range(CT):
                    th, tl = (t[:, f % 4, c * P:(c + 1) * P] for t in (hh, hl))
                    wh, wl = w2h[:, f % SLOTS2, :], w2l[:, f % SLOTS2, :]
                    nc.tensor.matmul(ps[:, c, :], th, wh, start=(f == 0), stop=False)
                    nc.tensor.matmul(ps[:, c, :], th, wl, start=False, stop=False)
                    last = nc.tensor.matmul(ps[:, c, :], tl, wh, start=False, stop=(f == KF - 1))
                last.then_inc(f_down, 1)

            halves = [0]

            def body(i, more):
                halves[0] = (i & 1) * EB if isinstance(i, int) else pe.snap((i & 1) * EB)
                for f in range(KF):
                    up(i, f)
                    q = i * KF + f if isinstance(i, int) else None
                    if at(i, 0) and f == 0:
                        pe.wait_ge(a_xn2, NBLK)
                        pe.wait_ge(v_gsub, NBLK - 1)
                        pe_xn2T((NBLK - 1) % 2)
                    if at(i, 0) and f == 1:
                        pe.wait_ge(a_xn2T, NBLK)
                        pe_gate(gate_sc7)
                    if q is not None and q - 1 in ROUNDS_AT:
                        pe_round(pe, 1, q - 1 - ROUNDS_AT[0])
                    if more and f == LOOKUP:
                        pe_lookup(pe, i + 1, BANK[1])
                    if q == CHOICE_AT + 1:
                        pe_before(pe, 1, 0)
                    if q == CHOICE_AT + 3:
                        pe_before(pe, 1, 1)
                    if f >= 2:
                        down(i, f - 2)
                    if more and f in TURNS:
                        transposes(i + 1, TURNS.index(f), 6)
                for f in range(KF - 2, KF):
                    down(i, f)

            pe.wait_ge(a_xn2T, NBLK - 1)
            pe_gate(gate_sc7)
            pe.wait_ge(v_gsub, NBLK - 2)
            for k in range(KD):
                transposes(0, k, k)
            columns(pe, body)
        with nc.Block() as block:
            @block.sync
            def _(sp):
                sp_attention(sp)
                sp_experts(sp)

            @block.gpsimd
            def _(pool):
                pool_attention(pool)
                pool_experts(pool)

            @block.scalar
            def _(act):
                act_attention(act)
                act_experts(act)

            @block.vector
            def _(dve):
                dve_attention(dve)
                dve_experts(dve)

            @block.tensor
            def _(pe):
                pe_attention(pe)
                pe_experts(pe)
        ffn.close()


_INS = ['x', 'ctx_768', 'L0_xattn_Wq', 'L0_xattn_Wk', 'L0_xattn_Wv', 'L0_xattn_Wo', 'L0_xattn_bo', 'L0_ffn_gate_w',
        'L0_ffn_w1', 'L0_ffn_w2']


def kernel(**inputs):
    import numpy as _np
    import concourse.bacc as _bacc
    from concourse import mybir as _mybir
    from concourse.bass_utils import run_bass_kernel_spmd as _run

    nc = _bacc.Bacc("TRN2", target_bir_lowering=False, num_devices=1)
    arrays, args = {}, []
    for name in _INS:
        a = _np.ascontiguousarray(inputs[name])
        arrays[f"in_{name}_dram"] = a
        args.append(nc.dram_tensor(f"in_{name}_dram", a.shape, _mybir.dt.from_np(a.dtype), kind="ExternalInput").ap())
    out = nc.dram_tensor("out_dram", (B, S, D), _mybir.dt.float32, kind="ExternalOutput").ap()
    xattn_expert_choice(nc, *args, out)
    r = _run(nc, [arrays], core_ids=[0])
    return r.results[0]["out_dram"]
```

```python
import concourse.bass as bass
from concourse import mybir
from concourse.alu_op_type import AluOpType as ALU
from contextlib import ExitStack

F32 = mybir.dt.float32
F32R = mybir.dt.float32r
BF16 = mybir.dt.bfloat16
U32 = mybir.dt.uint32
ACT = mybir.ActivationFunctionType
AX = mybir.AxisListType

P = 128
B, S, D = 2, 2048, 512
H, HD = 8, 64
J, CK = 77, 384
E, F = 8, 2048
CAP = 2 * S // E
KD, KC, KF = D // P, CK // P, F // P
HJ = H * J
HALF = HJ // 2
MAIN, REST = 6 * J, 2 * J
PAIR = 2 * J
CH = [(c * P, min(P, HJ - c * P)) for c in range(-(-HJ // P))]
NCH = len(CH)
WC = NCH * P
TPB = 2
NT = S // P
NBLK = B * NT // TPB
COLS = B * E
CT = CAP // P
EPS = 1e-5
CAND = 3
ROUNDS = 15
NV = 5


def xattn_expert_choice(nc, x, ctx, wq, wk, wv, wo, bo, gate_w, w1, w2, out):
    xn2_rows = nc.dram_tensor("xn2_rows", (B * S, D), F32, kind="Internal").ap()
    x_blk = x.rearrange("b (n t p) d -> (b n) p t d", t=TPB, p=P)
    out_blk = out.rearrange("b (n t p) d -> (b n) p t d", t=TPB, p=P)
    out_rows = out.rearrange("b s d -> (b s) d")
    xn2_blk = xn2_rows.rearrange("(n t p) d -> n p t d", t=TPB, p=P)

    top = ExitStack()
    with top:
        def sb(scope, name, shape, dt=F32):
            return scope.enter_context(nc.sbuf_tensor(name, shape, dt))

        def sem(name):
            return top.enter_context(nc.semaphore(name))

        ident = sb(top, "ident", [P, P])
        ones_bf = sb(top, "ones_bf", [P, P], BF16)
        before_bf = sb(top, "before_bf", [P, P], BF16)
        col_iota = sb(top, "col_iota", [P, P], BF16)
        quarter_iota = sb(top, "quarter_iota", [P, CT], BF16)
        part_iota = sb(top, "part_iota", [P, 1], BF16)
        tile_iota = sb(top, "tile_iota", [P, B, E, NT], BF16)
        eps_c = sb(top, "eps_c", [P, TPB])
        pow_c = sb(top, "pow_c", [P, TPB])
        minus_c = sb(top, "minus_c", [P, TPB])
        bo_rows = sb(top, "bo_rows", [P, TPB, D])
        gwT = sb(top, "gwT", [P, KD, E])
        probs = sb(top, "probs", [P, B, E, NT])
        tok_idx = sb(top, "tok_idx", [P, COLS, CT], U32)
        tok_gate = sb(top, "tok_gate", [P, COLS, CT])
        XB = sb(top, "XB", [P, 2, TPB, D])
        XN = sb(top, "XN", [P, TPB, D])
        xTh = sb(top, "xTh", [P, TPB, D], F32R)
        xTl = sb(top, "xTl", [P, TPB, D], F32R)
        st1 = sb(top, "st1", [P, TPB, 6])
        mv1 = sb(top, "mv1", [P, TPB, 2])
        rs1 = sb(top, "rs1", [P, TPB])
        ve1 = sb(top, "ve1", [P, TPB])
        nb1 = sb(top, "nb1", [P, TPB])
        st2 = sb(top, "st2", [P, TPB, 6])
        mv2 = sb(top, "mv2", [P, TPB, 2])
        rs2 = sb(top, "rs2", [P, TPB])
        ve2 = sb(top, "ve2", [P, TPB])
        nb2 = sb(top, "nb2", [P, TPB])
        gmax = sb(top, "gmax", [P, TPB])
        gexp = sb(top, "gexp", [P, TPB, E])
        gsub = sb(top, "gsub", [P, TPB, E])
        gsum = sb(top, "gsum", [P, TPB])
        grec = sb(top, "grec", [P, TPB])
        rows_in = XB[:].rearrange("p b t d -> p (b t) d")
        assert 2 * TPB == CT
        ps = top.enter_context(nc.psum_tensor("ps", [P, 8, 512], F32))
        thr = sb(top, "thr", [P, E])
        cand = sb(top, "cand", [P, E, CAND])
        bits = sb(top, "bits", [P, E, CAND])
        kept = sb(top, "kept", [P, E, CAND])
        best = sb(top, "best", [P, E])
        hit = sb(top, "hit", [P, E, CAND, NT], BF16)
        cnt = sb(top, "cnt", [P, E * CAND], BF16)
        above = sb(top, "above", [P, E, NT], BF16)
        tied = sb(top, "tied", [P, E, NT], BF16)
        chosen = sb(top, "chosen", [P, E, NT], BF16)
        room = sb(top, "room", [P, E])
        chain = sb(top, "chain", [P, E, NT])
        run = sb(top, "run", [P, E, NT])
        run2 = sb(top, "run2", [P, E, NT])
        place = sb(top, "place", [P, E, NT])
        q1 = sb(top, "q1", [P, E, NT])
        q2 = sb(top, "q2", [P, E, NT])
        quarter = sb(top, "quarter", [P, E, NT])
        row = sb(top, "row", [P, B, E, NT])
        rest1 = sb(top, "rest1", [P, E, NT])
        rest2 = sb(top, "rest2", [P, E, NT])
        gp = [sb(top, f"gp{i}", [P, E, NT], BF16) for i in range(3)]
        inq = sb(top, "inq", [P, E, NT, CT], BF16)
        vals = sb(top, "vals", [P, B, E, NT, NV, CT], BF16)
        hot = sb(top, "hot", [P, NT, P], BF16)
        found = sb(top, "found", [P, NV, CT])
        fsum = sb(top, "fsum", [P, CT])
        G, GF = 4, KF // 4
        gidx = sb(top, "gidx", [P, CT], U32)
        sidx = sb(top, "sidx", [P, CT], U32)
        w1_raw = sb(top, "w1_raw", [P, 2, KD, GF * P])
        w2_raw = sb(top, "w2_raw", [P, 2, GF, D])

        attn = ExitStack()
        AH = sb(attn, "AH", [P, B, KD, HJ], F32R)
        AL = sb(attn, "AL", [P, B, KD, HJ], F32R)
        BH = sb(attn, "BH", [P, B, NCH, D], F32R)
        BL = sb(attn, "BL", [P, B, NCH, D], F32R)
        init = ExitStack()
        ctx_sb = sb(init, "ctx_sb", [J, B, CK])
        gw_sb = sb(init, "gw_sb", [E, D])
        wq_sb = w1_raw[:, 1]
        wk_sb, wv_sb = w2_raw[:, 0, 0:KC], w2_raw[:, 1, 0:KC]
        wo_sb = w1_raw[:, 0]
        ctxT = sb(init, "ctxT", [P, KC, B, J])
        wqT = sb(init, "wqT", [P, KD, D])
        kx = sb(init, "kx", [P, B, KD, PAIR])
        vx = sb(init, "vx", [P, B, KD, WC])
        before_f = sb(init, "before_f", [P, P])

        c_ident = sem("c_ident")
        c_zero = sem("c_zero")
        c_const = sem("c_const")
        CONSTS = 9
        c_vx = sem("c_vx")
        d_ctx, d_gw, d_wk, d_wv, d_wq, d_wo, d_bo = (sem(f"d_{n}") for n in "ctx gw wk wv wq wo bo".split())
        p_ctxT = sem("p_ctxT")
        e_ctxT = sem("e_ctxT")
        p_kv = sem("p_kv")
        e_kv = sem("e_kv")
        p_wqT = sem("p_wqT")
        e_wqT = [sem(f"e_wqT{i}") for i in range(2)]
        p_fold = sem("p_fold")
        e_hi = sem("e_hi")
        e_lo = sem("e_lo")

        WQ_BANKS = (0, 1, 6, 7)
        NA = B * KD
        folds = [(kind, b, c) for kind, n in (("A", KD), ("B", NCH)) for b in range(B) for c in range(n)]

        def fold_bufs(n):
            kind, b, c = folds[n]
            if kind == "A":
                src = ps[:, 2 * (n % 4):2 * (n % 4) + 2, 0:HALF]
                hi, lo = (t[:, b, c, :].rearrange("p (h j) -> p h j", h=2) for t in (AH, AL))
            else:
                src = ps[:, 4 + n % 2, :]
                hi, lo = BH[:, b, c, :], BL[:, b, c, :]
            return src, hi, lo

        d_x = [sem(f"d_x{i}") for i in range(2)]
        d_xr = [sem(f"d_xr{i}") for i in range(2)]
        d_x1 = [sem(f"d_x1{i}") for i in range(2)]
        d_xn2 = [sem(f"d_xn2{i}") for i in range(2)]
        (v_st1, v_mv1, g_ve1, g_rs1, g_nb1, a_xn, p_xT, a_xTh, v_xTl, p_s, v_max, v_nmax, a_exp, v_rec, g_prob,
         p_pT, a_tails, v_tails, a_pTh, v_pTl, p_o, g_xr, v_x1, v_st2, v_mv2, g_ve2, g_rs2, g_nb2, a_xn2, p_xn2T,
         a_xn2T, p_g, v_gmax, v_gsub, a_gexp, v_gsum, v_grec, v_gate) = (sem(n) for n in (
             "v_st1 v_mv1 g_ve1 g_rs1 g_nb1 a_xn p_xT a_xTh v_xTl p_s v_max v_nmax a_exp v_rec g_prob "
             "p_pT a_tails v_tails a_pTh v_pTl p_o g_xr v_x1 v_st2 v_mv2 g_ve2 g_rs2 g_nb2 a_xn2 p_xn2T a_xn2T p_g "
             "v_gmax v_gsub a_gexp v_gsum v_grec v_gate").split())

        def sp_setup(sp):
            sp.dma_start(ctx_sb[:], ctx.rearrange("b j c -> j b c")).then_inc(d_ctx, 16)
            sp.dma_start(gw_sb[:], gate_w).then_inc(d_gw, 16)
            sp.dma_start(wk_sb, wk.rearrange("(c p) n -> p c n", p=P)).then_inc(d_wk, 16)
            sp.dma_start(XB[:, 0], x_blk[0]).then_inc(d_x[0], 16)
            sp.dma_start(wq_sb, wq.rearrange("(c p) n -> p c n", p=P)).then_inc(d_wq, 16)
            sp.dma_start(wv_sb, wv.rearrange("(c p) n -> p c n", p=P)).then_inc(d_wv, 16)
            sp.dma_start(wo_sb, wo.rearrange("(c p) n -> p c n", p=P)).then_inc(d_wo, 16)
            for t in range(TPB):
                sp.dma_start(bo_rows[:, t, :], bo.partition_broadcast(P)).then_inc(d_bo, 16)
            sp.dma_start(XB[:, 1], x_blk[1]).then_inc(d_x[1], 16)

        def pool_setup(pool):
            pool.memset(ident[:], 0.0).then_inc(c_zero, 1)
            pool.wait_ge(c_zero, 1)
            pool.affine_select(out=ident[:], in_=ident[:], compare_op=ALU.not_equal, fill=1.0, base=0,
                               pattern=[[-1, P]], channel_multiplier=1).then_inc(c_ident, 1)
            pool.memset(before_f[:], 1.0).then_inc(c_zero, 1)
            pool.wait_ge(c_zero, 2)
            pool.affine_select(out=before_bf[:], in_=before_f[:], compare_op=ALU.is_gt, fill=0.0, base=0,
                               pattern=[[1, P]], channel_multiplier=-1).then_inc(c_const, 1)
            pool.memset(ones_bf[:], 1.0).then_inc(c_const, 1)
            pool.memset(eps_c[:], EPS).then_inc(c_const, 1)
            pool.memset(pow_c[:], -0.5).then_inc(c_const, 1)
            pool.memset(minus_c[:], -1.0).then_inc(c_const, 1)
            pool.iota(col_iota[:], pattern=[[1, P]], base=0, channel_multiplier=0,
                      allow_small_or_imprecise_dtypes=True).then_inc(c_const, 1)
            pool.iota(quarter_iota[:], pattern=[[1, CT]], base=0, channel_multiplier=0,
                      allow_small_or_imprecise_dtypes=True).then_inc(c_const, 1)
            pool.iota(part_iota[:], pattern=[[0, 1]], base=0, channel_multiplier=1,
                      allow_small_or_imprecise_dtypes=True).then_inc(c_const, 1)
            pool.iota(tile_iota[:], pattern=[[NT, B], [0, E], [1, NT]], base=0, channel_multiplier=0,
                      allow_small_or_imprecise_dtypes=True).then_inc(c_const, 1)
            pool.wait_ge(c_const, CONSTS)
            pool_rstd(pool, mv1, ve1, rs1, nb1, v_mv1, g_ve1, g_rs1, g_nb1, a_xn, 0)
            pool.memset(vx[:], 0.0).then_inc(c_vx, 1)

        def pe_setup(pe):
            pe.wait_ge(c_ident, 1)
            pe.wait_ge(d_ctx, 16)
            for b in range(B):
                for c in range(KC):
                    nc.tensor.transpose(ps[:, 0, (c * B + b) * J:(c * B + b + 1) * J],
                                        ctx_sb[:, b, c * P:(c + 1) * P], ident[0:J, 0:J])
            pe.wait_ge(d_gw, 16)
            for c in range(KD):
                last = nc.tensor.transpose(ps[:, 1, c * E:(c + 1) * E], gw_sb[:, c * P:(c + 1) * P],
                                           ident[0:E, 0:E])
            last.then_inc(p_ctxT, 1)
            pe.wait_ge(e_ctxT, 1)
            for w, arrived, bank in ((wk_sb, d_wk, 2), (wv_sb, d_wv, 4)):
                pe.wait_ge(arrived, 16)
                for t in range(KD):
                    for c in range(KC):
                        last = nc.tensor.matmul(ps[:, bank + t // 2, (t % 2) * B * J:(t % 2 + 1) * B * J],
                                                w[:, c, t * P:(t + 1) * P],
                                                ctxT[:, c, :, :].rearrange("p b j -> p (b j)"),
                                                start=(c == 0), stop=(c == KC - 1))
                last.then_inc(p_kv, 1)
                if w is wk_sb:
                    pe.wait_ge(a_xn, 1)
                    pe_xT()
                    pe.wait_ge(d_wq, 16)
                    for t in range(KD):
                        if t == KD // 2:
                            pe.wait_ge(v_xTl, 1)
                        for dk in range(KD):
                            last = nc.tensor.transpose(ps[:, WQ_BANKS[t], dk * P:(dk + 1) * P],
                                                       wq_sb[:, dk, t * P:(t + 1) * P], ident[:])
                        last.then_inc(p_wqT, 1)
            pe.wait_ge(c_const, CONSTS)
            pe.wait_ge(e_kv, 1)
            for t in range(KD):
                pe.wait_ge(e_wqT[t % 2], t // 2 + 1)
            for n in range(NA):
                if n == 2:
                    pe.wait_ge(e_kv, 2)
                pe_fold(pe, n)

        def pe_fold(pe, n):
            kind, b, c = folds[n]
            if n >= 4:
                pe.wait_ge(e_lo, n - 3 if kind == "A" else max(n - 1, NA))
            if kind == "A":
                for t in range(KD):
                    last = nc.tensor.matmul(ps[:, 2 * (n % 4) + t // 2, (t % 2) * PAIR:(t % 2 + 1) * PAIR],
                                            wqT[:, t, c * P:(c + 1) * P], kx[:, b, t, :], start=True, stop=True)
            else:
                lo, hi = c * P, (c + 1) * P
                ts = [t for t in range(KD) if t * PAIR < hi and (t + 1) * PAIR > lo]
                for t in ts:
                    last = nc.tensor.matmul(fold_bufs(n)[0], vx[:, b, t, lo:hi], wo_sb[:, t, :],
                                            start=(t == ts[0]), stop=(t == ts[-1]))
            last.then_inc(p_fold, 1)

        def act_fold(act, n):
            act.wait_ge(p_fold, n + 1)
            src, hi, _ = fold_bufs(n)
            nc.scalar.activation(hi, src, ACT.Copy).then_inc(e_hi, 1)

        def dve_fold(dve, n):
            dve.wait_ge(e_hi, n + 1)
            src, hi, lo = fold_bufs(n)
            nc.vector.tensor_tensor(lo, src, hi.bitcast(F32), ALU.subtract).then_inc(e_lo, 1)

        def act_setup(act):
            act_normalise(act, XB[:, 0], rs1, nb1, XN, g_nb1, a_xn, 0)
            act_xTh(act, 0)
            for t in range(0, KD, 2):
                act.wait_ge(p_wqT, t + 1)
                nc.scalar.activation(wqT[:, t, :], ps[:, WQ_BANKS[t], :], ACT.Copy).then_inc(e_wqT[0], 1)
            for n in range(NA):
                act_fold(act, n)

        def dve_setup(dve):
            nc.vector.memset(kx[:], 0.0)
            dve.wait_ge(p_ctxT, 1)
            nc.vector.tensor_copy(gwT[:].rearrange("p c e -> p (c e)"), ps[:, 1, 0:KD * E])
            nc.vector.tensor_copy(ctxT[:].rearrange("p c b j -> p (c b j)"),
                                  ps[:, 0, 0:KC * B * J]).then_inc(e_ctxT, 1)
            dve.wait_ge(d_x[0], 16)
            stats(XB[:, 0], st1, v_st1)
            dve.wait_ge(v_st1, 1)
            aggregate(st1, mv1, v_mv1)
            dve.wait_ge(e_ctxT, 1)
            dve.wait_ge(c_const, CONSTS)
            for m, (dst, step, bank) in enumerate(((kx, 0, 2), (vx, PAIR, 4))):
                dve.wait_ge(p_kv, m + 1)
                if m == 1:
                    dve.wait_ge(c_vx, 1)
                for t in range(KD):
                    for h in range(2):
                        col = step * t + h * J
                        last = nc.vector.tensor_copy(
                            dst[h * HD:(h + 1) * HD, :, t, col:col + J],
                            ps[h * HD:(h + 1) * HD, bank + t // 2,
                               (t % 2) * B * J:(t % 2 + 1) * B * J].rearrange("p (b j) -> p b j", b=B))
                last.then_inc(e_kv, 1)
                if m == 0:
                    dve_xTl(dve, 0)
                    for t in range(1, KD, 2):
                        dve.wait_ge(p_wqT, t + 1)
                        nc.vector.tensor_copy(wqT[:, t, :], ps[:, WQ_BANKS[t], :]).then_inc(e_wqT[1], 1)
            for n in range(NA):
                dve_fold(dve, n)
        init.close()

        tiles = ExitStack()
        PR = sb(tiles, "PR", [P, TPB, H, J])
        nmax = sb(tiles, "nmax", [P, TPB, H])
        smax = sb(tiles, "smax", [P, TPB, H])
        ssum = sb(tiles, "ssum", [P, TPB * H])
        srec = sb(tiles, "srec", [P, TPB * H])
        XR = sb(tiles, "XR", [P, 2, TPB, D])
        pTh = sb(tiles, "pTh", [P, TPB, NCH, P], F32R)
        pTl = sb(tiles, "pTl", [P, TPB, NCH, P], F32R)
        X1 = sb(tiles, "X1", [P, 2, TPB, D])
        XN2 = sb(tiles, "XN2", [P, 2, TPB, D])
        xn2T = sb(tiles, "xn2T", [P, TPB, D])

        FIRST, LAST = -1, NBLK
        LOOP = (4, NBLK // B + 2)

        def steps(eng, body):
            for i in range(FIRST, LOOP[0]):
                body(i, i % 2, i // 2, lambda n: 0 <= n < NBLK)
            with eng.Fori(LOOP[0] // 2, LOOP[1] // 2, 1) as k:
                for u in range(2):
                    body(2 * k + u, u, k, lambda n: True)
            for i in range(LOOP[1], LAST + 1):
                body(i, i % 2, i // 2, lambda n: 0 <= n < NBLK)

        def transposed(i, has):
            return has(i + 1) and not at(i, -1)

        def tile_scores(t):
            return ps[:, 2 * t:2 * t + 2, 0:HALF].rearrange("p s (h j) -> p s h j", j=J)

        TAIL = CH[-1][1]
        tails = ps[0:TAIL, 1:3, HALF:HALF + P]
        gate_sc = ps[:, 3, HALF:HALF + TPB * E].rearrange("p (t e) -> p t e", e=E)
        gate_sc7 = ps[:, 7, 0:TPB * E].rearrange("p (t e) -> p t e", e=E)

        (s_init, s_bits, s_cand, s_hit, s_cnt, s_tot, s_kept, s_best, s_thr, s_link, s_mask, s_before, s_placed,
         s_vals, h_hot, h_used, h_found, h_fsum, h_idx) = (sem(n) for n in (
             "s_init s_bits s_cand s_hit s_cnt s_tot s_kept s_best s_thr s_link s_mask s_before s_placed "
             "s_vals h_hot h_used h_found h_fsum h_idx").split())
        SLOTS = 3
        GATED = NBLK // B + 2
        CHOICE = GATED + ROUNDS // SLOTS

        def at(i, n):
            return isinstance(i, int) and i == n

        def round_at(i, slot):
            if not isinstance(i, int):
                return None
            k = (i - GATED) * SLOTS + slot - (SLOTS - 1)
            return k if 0 <= k < ROUNDS else None

        def choice(bank):
            inside, sums = ps[:, bank, 128:128 + E * NT], ps[:, bank, 256:256 + E * NT]
            return inside, sums, ps[:, bank, 384:384 + E * CAND], ps[:, bank, 416:416 + NV * CT]

        BANK = (0, 7)

        def round_bank(b, k):
            return BANK[1] if b == 1 else 0 if k % SLOTS == 0 else 3

        chained = [0]

        def link(ins):
            chained[0] += 1
            ins.then_inc(s_link, 1)
            nc.vector.wait_ge(s_link, chained[0])

        def u32(t):
            return t[:].bitcast(U32)

        def spread(t):
            return t[:].unsqueeze(2).broadcast_to([P, E, NT])

        def each_cand(t):
            return t.unsqueeze(2).broadcast_to([P, E, CAND])

        def dve_narrow(dve, b, k):
            n = b * ROUNDS + k + 1
            counts = choice(round_bank(b, k))[2].rearrange("p (e m) -> p e m", m=CAND)
            dve.wait_ge(s_tot, n)
            nc.vector.scalar_tensor_tensor(out=kept[:], in0=counts, scalar=float(CAP), in1=cand[:],
                                           op0=ALU.is_ge, op1=ALU.mult).then_inc(s_kept, 1)
            dve.wait_ge(s_kept, n)
            nc.vector.tensor_reduce(best[:], kept[:], AX.X, ALU.max).then_inc(s_best, 1)
            dve.wait_ge(s_best, n)
            nc.vector.tensor_tensor(thr[:], thr[:], best[:], ALU.max).then_inc(s_thr, 1)

        def dve_round(dve, b, k):
            n = b * ROUNDS + k + 1
            if k == 0:
                dve.wait_ge(v_gate, (b + 1) * (NBLK // B))
                if b == 0:
                    nc.vector.memset(chain[:], 1.0)
                    link(nc.vector.memset(hit[:, 0, 0, 0:1], 0.0))
                    nc.vector.memset(chain[:, :, 0:1], 0.0)
                for m in range(CAND):
                    nc.vector.memset(bits[:, :, m:m + 1], 2.0 ** (32 * m - 95))
                nc.vector.memset(thr[:], 0.0).then_inc(s_init, 1)
                dve.wait_ge(s_init, b + 1)
            else:
                dve_narrow(dve, b, k - 1)
                dve.wait_ge(s_thr, n - 1)
                dve.wait_ge(s_bits, n - 1)
            nc.vector.tensor_tensor(u32(cand), each_cand(u32(thr)), u32(bits), ALU.bitwise_or).then_inc(s_cand, 1)
            dve.wait_ge(s_cand, n)
            shape = [P, E, CAND, NT]
            nc.vector.tensor_tensor(hit[:], probs[:, b].unsqueeze(2).broadcast_to(shape),
                                    cand[:].unsqueeze(3).broadcast_to(shape), ALU.is_ge).then_inc(s_hit, 1)
            nc.vector.tensor_scalar(u32(bits), u32(bits), 2, None, ALU.logical_shift_right).then_inc(s_bits, 1)
            dve.wait_ge(s_hit, n)
            with nc.allow_low_precision(reason="counts up to 16 are exact in bfloat16"):
                nc.vector.tensor_reduce(cnt[:], hit[:].rearrange("p e m t -> p (e m) t"), AX.X,
                                        ALU.add).then_inc(s_cnt, 1)

        def pe_round(pe, b, k):
            pe.wait_ge(s_cnt, b * ROUNDS + k + 1)
            nc.tensor.matmul(choice(round_bank(b, k))[2], ones_bf[:], cnt[:], start=True, stop=True).then_inc(s_tot, 1)

        def dve_masks(dve, b):
            dve_narrow(dve, b, ROUNDS - 1)
            dve.wait_ge(s_thr, (b + 1) * ROUNDS)
            nc.vector.tensor_tensor(tied[:], probs[:, b], spread(thr), ALU.is_equal)
            link(nc.vector.tensor_tensor(above[:], probs[:, b], spread(thr), ALU.is_gt))
            with nc.allow_low_precision(reason="counts up to 16 are exact in bfloat16"):
                nc.vector.tensor_reduce(cnt[:, 0:E], above[:], AX.X, ALU.add).then_inc(s_mask, 1)

        def pe_before(pe, b, m):
            pe.wait_ge(s_mask, 2 * b + m + 1)
            inside, sums, counts, _ = choice(BANK[b])
            if m == 0:
                nc.tensor.matmul(counts[:, 0:E], ones_bf[:], cnt[:, 0:E], start=True, stop=True)
            flat = (tied, chosen)[m][:].rearrange("p c t -> p (c t)")
            nc.tensor.matmul(inside, before_bf[:], flat, start=True, stop=True)
            nc.tensor.matmul(sums, ones_bf[:], flat, start=True, stop=True).then_inc(s_before, 1)

        def dve_places(dve, b, m):
            dve.wait_ge(s_before, 2 * b + m + 1)
            inside, sums, _, _ = choice(BANK[b])
            link(nc.vector.tensor_tensor_scan(run[:].rearrange("p c t -> p (c t)"),
                                              chain[:].rearrange("p c t -> p (c t)"), sums, 0.0, ALU.mult, ALU.add))
            link(nc.vector.tensor_tensor(run2[:], run[:], sums.rearrange("p (c t) -> p c t", t=NT), ALU.subtract))
            nc.vector.tensor_tensor(place[:], run2[:], inside.rearrange("p (c t) -> p c t", t=NT),
                                    ALU.add).then_inc(s_placed, 1)
            dve.wait_ge(s_placed, 2 * b + m + 1)

        def dve_chosen(dve, b):
            dve.wait_ge(s_before, 2 * b + 1)
            nc.vector.tensor_scalar(room[:], choice(BANK[b])[2][:, 0:E], -1.0, float(CAP), ALU.mult, ALU.add)
            dve_places(dve, b, 0)
            link(nc.vector.tensor_tensor(q1[:], place[:], spread(room), ALU.is_lt))
            link(nc.vector.tensor_tensor(q2[:], q1[:], tied[:], ALU.mult))
            nc.vector.tensor_tensor(chosen[:], q2[:], above[:], ALU.add).then_inc(s_mask, 1)

        def dve_gate_parts(b):
            prob = probs[:, b]
            link(nc.vector.tensor_copy(gp[0][:], prob))
            link(nc.vector.tensor_tensor(rest1[:], prob, gp[0][:], ALU.subtract))
            link(nc.vector.tensor_copy(gp[1][:], rest1[:]))
            link(nc.vector.tensor_tensor(rest2[:], rest1[:], gp[1][:], ALU.subtract))
            link(nc.vector.tensor_copy(gp[2][:], rest2[:]))

        def dve_rows(dve, b):
            link(nc.vector.tensor_scalar(q1[:], place[:], float(P), None, ALU.is_ge))
            link(nc.vector.scalar_tensor_tensor(out=q2[:], in0=place[:], scalar=float(2 * P), in1=q1[:],
                                                op0=ALU.is_ge, op1=ALU.add))
            link(nc.vector.scalar_tensor_tensor(out=quarter[:], in0=place[:], scalar=float(3 * P), in1=q2[:],
                                                op0=ALU.is_ge, op1=ALU.add))
            link(nc.vector.scalar_tensor_tensor(out=q1[:], in0=quarter[:], scalar=float(-P), in1=place[:],
                                                op0=ALU.mult, op1=ALU.add))
            link(nc.vector.scalar_tensor_tensor(out=q2[:], in0=q1[:], scalar=1.0, in1=chosen[:],
                                                op0=ALU.add, op1=ALU.mult))
            link(nc.vector.tensor_scalar(row[:, b], q2[:], -1.0, None, ALU.add))

        def dve_vals(b, e0, e1):
            n0, n1 = e0 * NT, e1 * NT
            shape = [P, n1 - n0, CT]

            def each(t):
                return t.unsqueeze(2).broadcast_to(shape)

            quarters = inq[:].rearrange("p c t q -> p (c t) q")[:, n0:n1, :]
            link(nc.vector.tensor_tensor(quarters, each(quarter[:].rearrange("p c t -> p (c t)")[:, n0:n1]),
                                         quarter_iota[:].unsqueeze(1).broadcast_to(shape), ALU.is_equal))
            numbers = [part_iota[:].broadcast_to([P, n1 - n0]), tile_iota[:, b].rearrange("p e t -> p (e t)")[:, n0:n1],
                       *(g[:].rearrange("p c t -> p (c t)")[:, n0:n1] for g in gp)]
            for v, number in enumerate(numbers):
                last = nc.vector.tensor_tensor(vals[:, b, e0:e1, :, v, :].rearrange("p c t q -> p (c t) q"),
                                               quarters, each(number), ALU.mult)
            last.then_inc(s_vals, 1)

        rows_flat = row[:].rearrange("p b c t -> p (b c t)")
        vals_flat = vals[:].rearrange("p b c t v q -> p (b c t v q)")
        flat_idx = tok_idx[:].rearrange("p c q -> p (c q)")
        flat_gate = tok_gate[:].rearrange("p c q -> p (c q)")

        def dve_one_hot(c):
            shape = [P, NT, P]
            nc.vector.tensor_tensor(hot[:], rows_flat[:, bass.ds(c * NT, NT)].unsqueeze(2).broadcast_to(shape),
                                    col_iota[:].unsqueeze(1).broadcast_to(shape), ALU.is_equal).then_inc(h_hot, 1)

        def pe_lookup(pe, c, bank):
            pe.wait_ge(h_hot, c + 1)
            for t in range(NT):
                last = nc.tensor.matmul(choice(bank)[3], hot[:, t, :],
                                        vals_flat[:, bass.ds(c * (NT * NV * CT) + t * NV * CT, NV * CT)],
                                        start=(t == 0), stop=(t == NT - 1))
            last.then_inc(h_used, 1)

        def dve_found(dve, c, bank):
            dve.wait_ge(h_used, c + 1)
            nc.vector.tensor_copy(found[:].rearrange("p v q -> p (v q)"), choice(bank)[3]).then_inc(h_found, 1)
            dve.wait_ge(h_found, c + 1)
            nc.vector.tensor_tensor(fsum[:], found[:, 2, :], found[:, 3, :], ALU.add).then_inc(h_fsum, 1)
            nc.vector.scalar_tensor_tensor(out=flat_idx[:, bass.ds(c * CT, CT)], in0=found[:, 1, :], scalar=float(P),
                                           in1=found[:, 0, :], op0=ALU.mult, op1=ALU.add)
            dve.wait_ge(h_fsum, c + 1)
            nc.vector.tensor_tensor(flat_gate[:, bass.ds(c * CT, CT)], fsum[:], found[:, 4, :],
                                    ALU.add).then_inc(h_idx, 1)

        f_raw = [sem(f"f_raw{i}") for i in range(2)]
        f_hh = sem("f_hh")
        f_passed = sem("f_passed")
        f_out = sem("f_out")
        (f_w1h, f_w2h, f_w1l, f_w2l, f_up, f_gelu, f_h, f_down, f_gidx, f_sidx, f_tr, f_eTh, f_eTl, f_ya, f_yd,
         f_yfree) = (sem(f"f_{n}") for n in
                     "w1h w2h w1l w2l up gelu h down gidx sidx tr eTh eTl ya yd yfree".split())
        f_rows = sem("f_rows")
        f_scat = sem("f_scat")
        w1_g = w1.rearrange("e (k p) f -> e p k f", p=P)
        w2_g = w2.rearrange("e (k p) d -> e p k d", p=P)

        def passed(eng, sem, value):
            eng.wait_ge(sem, value)
            eng.sem_inc(f_passed, 1)

        def sp_weights(sp, i, e, g, wait):
            a, b = w1_g[e, :, :, g * GF * P:(g + 1) * GF * P], w2_g[e, :, g * GF:(g + 1) * GF, :]
            if wait:
                passed(sp, f_w2l, i * KF + (g - 1) * GF)
            sp.dma_start(w1_raw[:, g % 2], a).then_inc(f_raw[g % 2], 16)
            sp.dma_start(w2_raw[:, g % 2], b).then_inc(f_raw[g % 2], 16)

        def sp_attention(sp):
            def step(i, u, has):
                if has(i + 4):
                    n, src = i + 4, x_blk[i + 4]
                    sp.wait_ge(a_xn, sp.snap(n - 1))
                    sp.dma_start(XB[:, u], src).then_inc(d_x[u], 16)
                if has(i - 2):
                    to1, to2, done = out_blk[i - 2], xn2_blk[i - 2], sp.snap(i - 1)
                    sp.wait_ge(v_x1, done)
                    sp.dma_start(to1, X1[:, u]).then_inc(d_x1[u], 16)
                    sp.wait_ge(a_xn2, done)
                    sp.dma_start(to2, XN2[:, u]).then_inc(d_xn2[u], 16)
                if has(i + 1):
                    n, src = i + 1, x_blk[i + 1]
                    free = sp.snap(n - 1)
                    if not isinstance(n, int) or n >= 2:
                        sp.wait_ge(v_x1, free)
                    sp.dma_start(XR[:, 1 - u], src).then_inc(d_xr[1 - u], 16)

            for i in range(-2, 4):
                if i == -1:
                    sp.wait_ge(p_fold, len(folds))
                step(i, i % 2, lambda n: 0 <= n < NBLK)
            with sp.Fori(2, NBLK // 2 - 2, 1) as k:
                for u in range(2):
                    step(2 * k + u, u, lambda n: True)
            for i in range(NBLK - 4, LAST + 1):
                step(i, i % 2, lambda n: 0 <= n < NBLK)
                if i == NBLK - 4:
                    for g in range(2):
                        sp_weights(sp, 0, 0, g, False)
            step(LAST + 1, (LAST + 1) % 2, lambda n: 0 <= n < NBLK)

        def pool_rstd(pool, mv, ve, rs, nb, ready, mid, scaled, done, used, n):
            pool.wait_ge(ready, n + 1)
            if not isinstance(n, int) or n > 0:
                pool.wait_ge(used, n)
            pool.tensor_tensor(nb[:], mv[:, :, 0], minus_c[:], ALU.mult)
            pool.tensor_tensor(ve[:], mv[:, :, 1], eps_c[:], ALU.add).then_inc(mid, 1)
            pool.wait_ge(mid, n + 1)
            pool.tensor_tensor(rs[:], ve[:], pow_c[:], ALU.pow).then_inc(scaled, 1)
            pool.wait_ge(scaled, n + 1)
            pool.tensor_tensor(nb[:], nb[:], rs[:], ALU.mult).then_inc(done, 1)

        def pool_gather(pool, i, first):
            if not first:
                passed(pool, f_rows, i * CT * 16)
            pool.wait_ge(h_idx, i + 1)
            pool.tensor_copy(gidx[:], flat_idx[:, bass.ds(i * CT, CT)]).then_inc(f_gidx, 1)
            passed(pool, f_gidx, i + 1)
            if first:
                pool.wait_ge(a_xn, NBLK)
                for u in range(2):
                    pool.wait_ge(d_xn2[u], 16 * NBLK // B // 2)
            else:
                passed(pool, f_tr, i * KD)
            src = xn2_rows[0:S, :] if first else xn2_rows
            for c in range(CT):
                pool.indirect_dma_start(out=rows_in[:, c, :], out_offset=None, in_=src,
                                        in_offset=bass.IndirectOffsetOnAxis(ap=gidx[:, c:c + 1], axis=0),
                                        ).then_inc(f_rows, 16)

        def pool_attention(pool):
            def step(i, u, half, has):
                if has(i - 1):
                    if at(i, 1):
                        pool.wait_ge(d_bo, 16 * TPB)
                    pool.wait_ge(d_xr[1 - u], 16 * half + 16 * u)
                    pool.tensor_tensor(XR[:, 1 - u], XR[:, 1 - u], bo_rows[:], ALU.add).then_inc(g_xr, 1)
                if at(i, NBLK):
                    pool_gather(pool, 0, True)
                if has(i - 2):
                    pool_rstd(pool, mv2, ve2, rs2, nb2, v_mv2, g_ve2, g_rs2, g_nb2, a_xn2, i - 2)
                if has(i + 2):
                    pool_rstd(pool, mv1, ve1, rs1, nb1, v_mv1, g_ve1, g_rs1, g_nb1, a_xn, i + 2)
                if has(i):
                    for t in range(TPB):
                        pool.wait_ge(v_rec, 2 * i + t + 1)
                        over = srec[:, t * H:(t + 1) * H].unsqueeze(2).broadcast_to([P, H, J])
                        pool.tensor_tensor(PR[:, t], PR[:, t], over, ALU.mult).then_inc(g_prob, 1)
            steps(pool, step)

        def act_gate_exp(act, n):
            act.wait_ge(v_gsub, n + 1)
            nc.scalar.activation(gexp[:], gsub[:], ACT.Exp).then_inc(a_gexp, 1)

        def act_xn2T(act, n):
            act.wait_ge(p_xn2T, n + 1)
            nc.scalar.activation(xn2T[:], ps[:, 6:8, :], ACT.Copy).then_inc(a_xn2T, 1)

        def act_normalise(act, src, rs, nb, dst, ready, done, n):
            act.wait_ge(ready, n + 1)
            for t in range(TPB):
                last = nc.scalar.activation(dst[:, t, :], src[:, t, :], ACT.Identity, bias=nb[:, t:t + 1],
                                            scale=rs[:, t:t + 1])
            last.then_inc(done, 1)

        def act_xTh(act, n):
            act.wait_ge(p_xT, n + 1)
            nc.scalar.activation(xTh[:], ps[:, 6:8, :], ACT.Copy).then_inc(a_xTh, 1)

        def act_attention(act):
            def exp(i, t):
                act.wait_ge(v_nmax, 2 * i + t + 1)
                for h in range(H):
                    last = nc.scalar.activation(PR[:, t, h, :], tile_scores(t)[:, h // 4, h % 4, :], ACT.Exp,
                                                bias=nmax[:, t, h:h + 1], scale=HD ** -0.5,
                                                accum_out=ssum[:, t * H + h:t * H + h + 1])
                last.then_inc(a_exp, 1)

            def step(i, u, half, has):
                if has(i - 1):
                    act.wait_ge(p_pT, i)
                    nc.scalar.activation(pTh[0:TAIL, :, NCH - 1, :], tails, ACT.Copy).then_inc(a_tails, 1)
                    nc.scalar.activation(pTh[:, :, 0:NCH - 1, :],
                                         ps[:, 6:8, :].rearrange("p t (c q) -> p t c q", q=P),
                                         ACT.Copy).then_inc(a_pTh, 1)
                if has(i - 3):
                    act_gate_exp(act, i - 3)
                if has(i):
                    exp(i, 0)
                if transposed(i, has):
                    act_xTh(act, i + 1)
                if has(i - 2):
                    if not isinstance(i, int) or i >= 4:
                        act.wait_ge(d_xn2[u], 16 * half - 16)
                    act_normalise(act, X1[:, u], rs2, nb2, XN2[:, u], g_nb2, a_xn2, i - 2)
                if has(i):
                    exp(i, 1)
                if at(i, 0):
                    for n in range(NA, len(folds)):
                        act_fold(act, n)
                if has(i + 2):
                    act_normalise(act, XB[:, u], rs1, nb1, XN, g_nb1, a_xn, i + 2)
                if has(i - 2) and not at(i, NBLK):
                    act_xn2T(act, i - 2)
            steps(act, step)

        def stats(src, st, done):
            for t in range(TPB):
                last = nc.vector.bn_stats(st[:, t, :], src[:, t, :])
            last.then_inc(done, 1)

        def aggregate(st, mv, done):
            for t in range(TPB):
                last = nc.vector.bn_aggr(mv[:, t, :], st[:, t, :])
            last.then_inc(done, 1)

        def dve_gate_scores(dve, n, scores):
            dve.wait_ge(p_g, n + 1)
            nc.vector.tensor_reduce(gmax[:], scores, AX.X, ALU.max).then_inc(v_gmax, 1)
            dve.wait_ge(v_gmax, n + 1)
            nc.vector.tensor_tensor(gsub[:], scores, gmax[:].unsqueeze(2).broadcast_to([P, TPB, E]),
                                    ALU.subtract).then_inc(v_gsub, 1)

        def dve_gate(dve, n):
            dve.wait_ge(a_gexp, n + 1)
            nc.vector.tensor_reduce(gsum[:], gexp[:], AX.X, ALU.add).then_inc(v_gsum, 1)
            dve.wait_ge(v_gsum, n + 1)
            nc.vector.reciprocal(grec[:], gsum[:]).then_inc(v_grec, 1)
            dve.wait_ge(v_grec, n + 1)
            b, pair = n // (NBLK // B), n % (NBLK // B) if isinstance(n, int) else n & (NBLK // B - 1)
            flat = probs[:].rearrange("p b e t -> p (b e t)")
            for t in range(TPB):
                to = b * (E * NT) + pair * TPB + t
                last = nc.vector.tensor_scalar(flat[:, bass.ds(to, E, step=NT)], gexp[:, t, :],
                                               grec[:, t:t + 1], None, ALU.mult)
            last.then_inc(v_gate, 1)

        def dve_x1(dve, n, u, stored):
            dve.wait_ge(p_o, n + 1)
            dve.wait_ge(g_xr, n + 1)
            if stored is not None:
                dve.wait_ge(d_x1[u], stored)
            nc.vector.tensor_tensor(X1[:, u], ps[:, 4:6, :], XR[:, u], ALU.add).then_inc(v_x1, 1)

        def dve_xTl(dve, n):
            dve.wait_ge(a_xTh, n + 1)
            nc.vector.tensor_tensor(xTl[:], ps[:, 6:8, :], xTh[:].bitcast(F32), ALU.subtract).then_inc(v_xTl, 1)

        def dve_attention(dve):
            def reciprocals(i):
                for t in range(TPB):
                    dve.wait_ge(a_exp, 2 * i + t + 1)
                    nc.vector.reciprocal(srec[:, t * H:(t + 1) * H],
                                         ssum[:, t * H:(t + 1) * H]).then_inc(v_rec, 1)

            def maximum(i, t):
                dve.wait_ge(p_s, 2 * i + t + 1)
                nc.vector.tensor_reduce(smax[:, t, :].rearrange("p (s h) -> p s h", s=2), tile_scores(t),
                                        AX.X, ALU.max).then_inc(v_max, 1)
                dve.wait_ge(v_max, 2 * i + t + 1)
                nc.vector.tensor_scalar(nmax[:, t, :], smax[:, t, :], -HD ** -0.5, None,
                                        ALU.mult).then_inc(v_nmax, 1)

            def step(i, u, half, has):
                if round_at(i, 0) is not None:
                    dve_round(dve, 0, round_at(i, 0))
                if at(i, CHOICE + 1):
                    dve_places(dve, 0, 1)
                    dve_rows(dve, 0)
                if has(i - 1):
                    dve.wait_ge(a_tails, i)
                    nc.vector.tensor_tensor(pTl[0:TAIL, :, NCH - 1, :], tails,
                                            pTh[0:TAIL, :, NCH - 1, :].bitcast(F32),
                                            ALU.subtract).then_inc(v_tails, 1)
                    dve.wait_ge(a_pTh, i)
                    nc.vector.tensor_tensor(pTl[:, :, 0:NCH - 1, :],
                                            ps[:, 6:8, :].rearrange("p t (c q) -> p t c q", q=P),
                                            pTh[:, :, 0:NCH - 1, :].bitcast(F32), ALU.subtract).then_inc(v_pTl, 1)
                if round_at(i, 1) is not None:
                    dve_round(dve, 0, round_at(i, 1))
                if has(i - 3) and not at(i, CHOICE + 1):
                    dve_gate_scores(dve, i - 3, gate_sc)
                if has(i - 2):
                    dve_x1(dve, i - 2, u, 16 * half - 16 if not isinstance(i, int) or i >= 4 else None)
                if at(i, CHOICE + 1):
                    dve_vals(0, 0, 1)
                    dve_one_hot(0)
                    dve_found(dve, 0, BANK[0])
                    dve_gate_scores(dve, i - 3, gate_sc)
                if has(i):
                    maximum(i, 0)
                if has(i - 2):
                    dve.wait_ge(v_x1, i - 1)
                    stats(X1[:, u], st2, v_st2)
                if has(i + 2):
                    dve.wait_ge(d_x[u], 16 * half + 32)
                    if has(i + 1):
                        dve.wait_ge(g_nb1, i + 2)
                    if has(i - 2):
                        dve.wait_ge(v_st2, i - 1)
                    stats(XB[:, u], st1, v_st1)
                elif has(i - 2):
                    dve.wait_ge(v_st2, i - 1)
                if has(i - 2):
                    aggregate(st2, mv2, v_mv2)
                if has(i + 2):
                    dve.wait_ge(v_st1, i + 3)
                if at(i, CHOICE):
                    dve.wait_ge(p_s, 2 * i + 2)
                    dve_masks(dve, 0)
                if has(i):
                    maximum(i, 1)
                if has(i + 2):
                    aggregate(st1, mv1, v_mv1)
                if has(i - 3):
                    dve_gate(dve, i - 3)
                if transposed(i, has):
                    dve_xTl(dve, i + 1)
                if has(i):
                    reciprocals(i)
                if at(i, 0):
                    for n in range(NA, len(folds)):
                        dve_fold(dve, n)
                if round_at(i, 2) is not None:
                    dve_round(dve, 0, round_at(i, 2))
                if at(i, GATED + 1):
                    dve_gate_parts(0)
                if at(i, CHOICE):
                    dve_chosen(dve, 0)
            steps(dve, step)
            dve_x1(dve, NBLK - 1, (NBLK - 1) % 2, 16 * (NBLK // 2 - 1))
            dve.wait_ge(v_x1, NBLK)
            stats(X1[:, (NBLK - 1) % 2], st2, v_st2)
            dve.wait_ge(g_nb2, NBLK - 1)
            dve.wait_ge(v_st2, NBLK)
            aggregate(st2, mv2, v_mv2)

        def pe_xT():
            for t in range(TPB):
                for dk in range(KD):
                    last = nc.tensor.transpose(ps[:, 6 + t, dk * P:(dk + 1) * P],
                                               XN[:, t, dk * P:(dk + 1) * P], ident[:])
            last.then_inc(p_xT, 1)

        def pe_gate(scores):
            for t in range(TPB):
                for dk in range(KD):
                    last = nc.tensor.matmul(scores[:, t, :], xn2T[:, t, dk * P:(dk + 1) * P], gwT[:, dk, :],
                                            start=(dk == 0), stop=(dk == KD - 1))
            last.then_inc(p_g, 1)

        def pe_xn2T(u):
            for t in range(TPB):
                for dk in range(KD):
                    last = nc.tensor.transpose(ps[:, 6 + t, dk * P:(dk + 1) * P],
                                               XN2[:, u, t, dk * P:(dk + 1) * P], ident[:])
            last.then_inc(p_xn2T, 1)

        def pe_attention(pe):
            def three(psum, pairs, **kw):
                n = len(pairs)
                for k, (wh, wl, mh, ml) in enumerate(pairs):
                    nc.tensor.matmul(psum, wh, mh, start=(k == 0), stop=False, **kw)
                    nc.tensor.matmul(psum, wh, ml, start=False, stop=False, **kw)
                    last = nc.tensor.matmul(psum, wl, mh, start=False, stop=(k == n - 1), **kw)
                return last

            def second_norm(i, u, has):
                pe.wait_ge(a_xn2, i - 1)
                if has(i + 1):
                    pe.wait_ge(v_xTl, i + 2)
                pe_xn2T(u)

            def step(i, u, half, has):
                if round_at(i - 1, 2) is not None:
                    pe_round(pe, 0, round_at(i - 1, 2))
                if at(i, CHOICE + 1):
                    pe_before(pe, 0, 1)
                if has(i - 1):
                    pe.wait_ge(g_prob, 2 * i - 1)
                    if has(i - 3):
                        pe.wait_ge(a_xn2T, i - 2)
                    elif has(i):
                        pe.wait_ge(v_xTl, i + 1)
                    flat = PR[:].rearrange("p t h j -> p (t h j)")
                    for t in range(TPB):
                        if t:
                            pe.wait_ge(g_prob, 2 * i)
                        for c, (c0, n) in enumerate(CH):
                            dst = tails[:, t, :] if c == NCH - 1 else ps[:, 6 + t, c0:c0 + P]
                            last = nc.tensor.transpose(dst, flat[:, t * HJ + c0:t * HJ + c0 + n], ident[:])
                    last.then_inc(p_pT, 1)
                if has(i - 3):
                    pe.wait_ge(a_xn2T, i - 2)
                    pe_gate(gate_sc)
                if round_at(i, 0) is not None:
                    pe_round(pe, 0, round_at(i, 0))
                if at(i, 0):
                    pe.wait_ge(e_lo, NA)
                if has(i):
                    pe.wait_ge(v_xTl, i + 1)
                    if isinstance(i, int):
                        batch = i // (NBLK // B)
                        base = [batch * KD * HJ + dk * HJ for dk in range(KD)]
                    else:
                        base0 = pe.snap(i // (NBLK // B) * (KD * HJ))
                        base = [base0 + dk * HJ for dk in range(KD)]
                    fh, fl = (m[:].rearrange("p b k n -> p (b k n)") for m in (AH, AL))
                    for t in range(TPB):
                        for part in range(2):
                            if has(i - 1) and (t, part) == (0, 1):
                                pe.wait_ge(v_tails, i)
                            if has(i - 3) and (t, part) == (1, 1):
                                pe.wait_ge(v_gsub, i - 2)
                            if round_at(i, 1) is not None and (t, part) == (1, 1):
                                pe_round(pe, 0, round_at(i, 1))
                            last = three(ps[:, 2 * t + part, 0:HALF],
                                         [(xTh[:, t, dk * P:(dk + 1) * P], xTl[:, t, dk * P:(dk + 1) * P],
                                           fh[:, bass.ds(base[dk] + part * HALF, HALF)],
                                           fl[:, bass.ds(base[dk] + part * HALF, HALF)])
                                          for dk in range(KD)])
                        last.then_inc(p_s, 1)
                if transposed(i, has):
                    pe.wait_ge(a_xn, i + 2)
                    if has(i - 1):
                        pe.wait_ge(v_pTl, i)
                    pe_xT()
                if at(i, 0):
                    pe.wait_ge(d_wo, 16)
                    for n in range(NA, len(folds)):
                        pe_fold(pe, n)
                if has(i - 1):
                    if at(i, 1):
                        pe.wait_ge(e_lo, len(folds))
                    pe.wait_ge(v_pTl, i)
                    if has(i - 2):
                        pe.wait_ge(v_x1, i - 1)
                    n = i - 1
                    if isinstance(n, int):
                        batch = n // (NBLK // B)
                        base = [(batch * NCH + c) * D for c in range(NCH)]
                    else:
                        base0 = pe.snap(n // (NBLK // B) * (NCH * D))
                        base = [base0 + c * D for c in range(NCH)]
                    fh, fl = (m[:].rearrange("p b k n -> p (b k n)") for m in (BH, BL))
                    for t in range(TPB):
                        last = three(ps[:, 4 + t, :],
                                     [(pTh[0:k, t, c, :], pTl[0:k, t, c, :],
                                       fh[0:k, bass.ds(base[c], D)], fl[0:k, bass.ds(base[c], D)])
                                      for c, (_, k) in enumerate(CH)])
                        if t == 0 and has(i - 2) and not at(i, NBLK):
                            second_norm(i, u, has)
                        if t == 0 and at(i, CHOICE):
                            pe.wait_ge(a_exp, 2 * i + 1)
                            pe_before(pe, 0, 0)
                        if t == 0 and at(i, CHOICE + 1):
                            pe.wait_ge(s_vals, 1)
                            pe_lookup(pe, 0, BANK[0])
                    last.then_inc(p_o, 1)
                elif has(i - 2):
                    second_norm(i, u, has)
            steps(pe, step)
        tiles.close()
        attn.close()

        ffn = ExitStack()
        SLOTS1, SLOTS2 = 4, 8
        w1h = sb(ffn, "w1h", [P, SLOTS1, KD, P], F32R)
        w1l = sb(ffn, "w1l", [P, SLOTS1, KD, P], F32R)
        w2h = sb(ffn, "w2h", [P, SLOTS2, D], F32R)
        w2l = sb(ffn, "w2l", [P, SLOTS2, D], F32R)
        eTh = sb(ffn, "eTh", [P, 2, KD, CAP], F32R)
        eTl = sb(ffn, "eTl", [P, 2, KD, CAP], F32R)
        hf = sb(ffn, "hf", [P, 2, CAP])
        hh = sb(ffn, "hh", [P, 4, CAP], F32R)
        hl = sb(ffn, "hl", [P, 4, CAP], F32R)
        Y = sb(ffn, "Y", [P, CT, D])

        flat_eTh = eTh[:].rearrange("p b k n -> p (b k n)")
        flat_eTl = eTl[:].rearrange("p b k n -> p (b k n)")
        EB = KD * CAP

        def columns(eng, body):
            body(0, True)
            body(1, True)
            with eng.Fori(2, COLS - 1, 1) as i:
                body(i, True)
            body(COLS - 1, False)

        LOOKUP = 3
        ROUNDS_AT = tuple(q for q in range(3, 5 + KF) if not KF <= q < KF + LOOKUP)[:ROUNDS]
        CHOICE_AT = ROUNDS_AT[-1] + 1
        assert len(ROUNDS_AT) == ROUNDS
        TURNS = tuple(range(KF // 2, KF, 2))

        def sp_experts(sp):
            for g in range(2, G):
                sp_weights(sp, 0, 0, g, True)
            with sp.Fori(1, COLS, 1) as i:
                for g in range(G):
                    sp_weights(sp, i, i & (E - 1), g, True)

        def pool_experts(pool):
            def body(i, more):
                if more:
                    pool_gather(pool, i + 1, False)
                pool.tensor_copy(sidx[:], flat_idx[:, bass.ds(i * CT, CT)]).then_inc(f_sidx, 1)
                passed(pool, f_sidx, i + 1)
                for c in range(CT):
                    if c < CT // 2:
                        passed(pool, f_yd, i * (CT // 2) + c + 1)
                    else:
                        passed(pool, f_ya, i * (CT // 2) + c - CT // 2 + 1)
                    pool.indirect_dma_start(out=out_rows,
                                            out_offset=bass.IndirectOffsetOnAxis(ap=sidx[:, c:c + 1], axis=0),
                                            in_=Y[:, c, :], in_offset=None, compute_op=ALU.add,
                                            ).then_inc(f_scat, 16)
                passed(pool, f_scat, (i + 1) * CT * 16)
                pool.sem_inc(f_yfree, 1)

            pool_rstd(pool, mv2, ve2, rs2, nb2, v_mv2, g_ve2, g_rs2, g_nb2, a_xn2, NBLK - 1)
            for u in range(2):
                pool.wait_ge(d_xn2[u], 16 * NBLK // 2)
                pool.wait_ge(d_x1[u], 16 * NBLK // 2)
            columns(pool, body)

        def act_experts(act):
            def weights(i, f, wait1, wait2):
                g, j = divmod(f, GF)
                if j == 0:
                    act.wait_ge(f_raw[g % 2], 64 * i + 32 * (g // 2 + 1))
                if wait1 is not None:
                    act.wait_ge(f_up, wait1)
                nc.scalar.activation(w1h[:, f % SLOTS1], w1_raw[:, g % 2, :, j * P:(j + 1) * P],
                                     ACT.Copy).then_inc(f_w1h, 1)
                if wait2 is not None:
                    act.wait_ge(f_down, wait2)
                nc.scalar.activation(w2h[:, f % SLOTS2], w2_raw[:, g % 2, j, :], ACT.Copy).then_inc(f_w2h, 1)

            def token_chunk(i, k, bank):
                act.wait_ge(f_tr, i * KD + k + 1)
                half = (i & 1) * EB
                nc.scalar.activation(flat_eTh[:, bass.ds(half + k * CAP, CAP)], ps[:, bank, :],
                                     ACT.Copy).then_inc(f_eTh, 1)

            def body(i, more):
                for f in range(KF):
                    if f + 2 < KF:
                        weights(i, f + 2, i * KF + f - 1 if f >= 2 else None,
                                i * KF + f - 5 if f >= 6 else None)
                    elif more:
                        weights(i + 1, f + 2 - KF, i * KF + f - 1, i * KF + f - 5)
                    act.wait_ge(f_up, i * KF + f + 1)
                    if f >= 2:
                        act.wait_ge(f_h, i * KF + f - 1)
                    nc.scalar.activation(hf[:, f % 2, :], ps[:, 4 + f % 2, :], ACT.Gelu).then_inc(f_gelu, 1)
                    if at(i, 0) and f == 0:
                        u = (NBLK - 1) % 2
                        act.wait_ge(d_xn2[u], 16 * (NBLK // 2 - 1))
                        act_normalise(act, X1[:, u], rs2, nb2, XN2[:, u], g_nb2, a_xn2, NBLK - 1)
                    if at(i, 0) and f == 1:
                        act_gate_exp(act, NBLK - 2)
                        act_xn2T(act, NBLK - 1)
                    if at(i, 0) and f == 3:
                        act_gate_exp(act, NBLK - 1)
                    if more and f - 1 in TURNS:
                        token_chunk(i + 1, TURNS.index(f - 1), 6)
                act.wait_ge(f_yfree, i + 1)
                for c in range(CT // 2, CT):
                    if c < CT - 1:
                        act.wait_ge(f_out, i * (CT - 1) + c + 1)
                    else:
                        act.wait_ge(f_down, (i + 1) * KF)
                    nc.scalar.activation(Y[:, c, :], ps[:, c, :], ACT.Copy,
                                         scale=flat_gate[:, bass.ds(i * CT + c, 1)]).then_inc(f_ya, 1)

            act.wait_ge(p_o, NBLK)
            for f in range(2):
                weights(0, f, None, None)
            for k in range(KD):
                token_chunk(0, k, k)
            act_xn2T(act, NBLK - 2)
            columns(act, body)

        def dve_experts(dve):
            def weights(f, n):
                g, j = divmod(f, GF)
                dve.wait_ge(f_w1h, n + 1)
                nc.vector.tensor_tensor(w1l[:, f % SLOTS1], w1_raw[:, g % 2, :, j * P:(j + 1) * P],
                                        w1h[:, f % SLOTS1].bitcast(F32), ALU.subtract).then_inc(f_w1l, 1)
                dve.wait_ge(f_w2h, n + 1)
                nc.vector.tensor_tensor(w2l[:, f % SLOTS2], w2_raw[:, g % 2, j, :],
                                        w2h[:, f % SLOTS2].bitcast(F32), ALU.subtract).then_inc(f_w2l, 1)

            def token_chunk(i, k, bank):
                dve.wait_ge(f_eTh, i * KD + k + 1)
                chunk = bass.ds((i & 1) * EB + k * CAP, CAP)
                nc.vector.tensor_tensor(flat_eTl[:, chunk], ps[:, bank, :], flat_eTh[:, chunk].bitcast(F32),
                                        ALU.subtract).then_inc(f_eTl, 1)

            def body(i, more):
                for f in range(KF):
                    if f + 2 < KF or more:
                        weights((f + 2) % KF, i * KF + f + 2)
                    dve.wait_ge(f_gelu, i * KF + f + 1)
                    if f >= 4:
                        dve.wait_ge(f_down, i * KF + f - 3)
                    nc.vector.tensor_copy(hh[:, f % 4], hf[:, f % 2, :]).then_inc(f_hh, 1)
                    dve.wait_ge(f_hh, i * KF + f + 1)
                    nc.vector.tensor_tensor(hl[:, f % 4], hf[:, f % 2, :], hh[:, f % 4].bitcast(F32),
                                            ALU.subtract).then_inc(f_h, 1)
                    if more and f == LOOKUP - 2:
                        dve_one_hot(i + 1)
                    if more and f == LOOKUP:
                        dve_found(dve, i + 1, BANK[1])
                    if at(i, 0) and f == 0:
                        dve_gate_scores(dve, NBLK - 2, gate_sc7)
                        dve_vals(0, 1, E)
                    if at(i, 0) and f == 1:
                        dve_gate(dve, NBLK - 2)
                    if at(i, 0) and f == 2:
                        dve_gate_scores(dve, NBLK - 1, gate_sc7)
                    if at(i, 0) and f == 3:
                        dve_gate(dve, NBLK - 1)
                    q = i * KF + f if isinstance(i, int) else None
                    if q in ROUNDS_AT:
                        dve_round(dve, 1, ROUNDS_AT.index(q))
                    if q == CHOICE_AT:
                        dve_masks(dve, 1)
                    if q == CHOICE_AT + 3:
                        dve_chosen(dve, 1)
                    if q == CHOICE_AT + 5:
                        dve_places(dve, 1, 1)
                        dve_rows(dve, 1)
                    if q == CHOICE_AT + 7:
                        dve_gate_parts(1)
                    if q == CHOICE_AT + 8:
                        dve_vals(1, 0, E)
                    if more and f - 1 in TURNS:
                        token_chunk(i + 1, TURNS.index(f - 1), 6)
                dve.wait_ge(f_yfree, i + 1)
                for c in range(CT // 2):
                    dve.wait_ge(f_out, i * (CT - 1) + c + 1)
                    nc.vector.tensor_scalar(Y[:, c, :], ps[:, c, :], flat_gate[:, bass.ds(i * CT + c, 1)],
                                            None, ALU.mult).then_inc(f_yd, 1)

            dve.sem_inc(f_yfree, 1)
            for f in range(2):
                weights(f, f)
            for k in range(KD):
                token_chunk(0, k, k)
            columns(dve, body)

        def pe_experts(pe):
            def transposes(i, k, bank):
                if k == 0:
                    pe.wait_ge(f_rows, 16 * CT * (i + 1))
                if bank == 6:
                    pe.wait_ge(f_eTl, i * KD + k)
                for c in range(CT):
                    last = nc.tensor.transpose(ps[:, bank, c * P:(c + 1) * P],
                                               rows_in[:, c, k * P:(k + 1) * P], ident[:])
                last.then_inc(f_tr, 1)

            def up(i, f, half):
                pe.wait_ge(f_w1l, i * KF + f + 1)
                if f == 0:
                    pe.wait_ge(f_eTl, (i + 1) * KD)
                if at(i, 0) and f == 0:
                    pe.wait_ge(v_x1, NBLK)
                if f >= 2:
                    pe.wait_ge(f_gelu, i * KF + f - 1)
                for k in range(KD):
                    chunk = bass.ds(half + k * CAP, CAP)
                    wh, wl = w1h[:, f % SLOTS1, k, :], w1l[:, f % SLOTS1, k, :]
                    nc.tensor.matmul(ps[:, 4 + f % 2, :], wh, flat_eTh[:, chunk], start=(k == 0), stop=False)
                    nc.tensor.matmul(ps[:, 4 + f % 2, :], wh, flat_eTl[:, chunk], start=False, stop=False)
                    last = nc.tensor.matmul(ps[:, 4 + f % 2, :], wl, flat_eTh[:, chunk], start=False,
                                            stop=(k == KD - 1))
                last.then_inc(f_up, 1)

            def down(i, f):
                pe.wait_ge(f_h, i * KF + f + 1)
                pe.wait_ge(f_w2l, i * KF + f + 1)
                for c in range(CT):
                    th, tl = (t[:, f % 4, c * P:(c + 1) * P] for t in (hh, hl))
                    wh, wl = w2h[:, f % SLOTS2, :], w2l[:, f % SLOTS2, :]
                    nc.tensor.matmul(ps[:, c, :], th, wh, start=(f == 0), stop=False)
                    nc.tensor.matmul(ps[:, c, :], th, wl, start=False, stop=False)
                    last = nc.tensor.matmul(ps[:, c, :], tl, wh, start=False, stop=(f == KF - 1))
                    if f == KF - 1 and c < CT - 1:
                        last.then_inc(f_out, 1)
                last.then_inc(f_down, 1)

            def body(i, more):
                half = (i & 1) * EB if isinstance(i, int) else pe.snap((i & 1) * EB)
                for f in range(KF):
                    up(i, f, half)
                    q = i * KF + f if isinstance(i, int) else None
                    if at(i, 0) and f in (0, 2):
                        pe.wait_ge(a_xn2T, NBLK - 1 + f // 2)
                        pe_gate(gate_sc7)
                    if at(i, 0) and f == 1:
                        pe.wait_ge(a_xn2, NBLK)
                        pe.wait_ge(v_gsub, NBLK - 1)
                        pe_xn2T((NBLK - 1) % 2)
                    if q is not None and q - 1 in ROUNDS_AT:
                        pe_round(pe, 1, ROUNDS_AT.index(q - 1))
                    if at(i, 0) and f == LOOKUP:
                        pe.wait_ge(v_gsub, NBLK)
                    if more and f == LOOKUP:
                        pe_lookup(pe, i + 1, BANK[1])
                    if q == CHOICE_AT + 2:
                        pe.wait_ge(h_found, 3)
                        pe_before(pe, 1, 0)
                    if q == CHOICE_AT + 4:
                        pe_before(pe, 1, 1)
                    if f >= 2:
                        down(i, f - 2)
                    if more and f in TURNS:
                        transposes(i + 1, TURNS.index(f), 6)
                for f in range(KF - 2, KF):
                    down(i, f)

            pe.wait_ge(v_gsub, NBLK - 2)
            for k in range(KD):
                transposes(0, k, k)
            pe.wait_ge(a_xn2, NBLK - 1)
            pe_xn2T((NBLK - 2) % 2)
            columns(pe, body)

        with nc.Block() as block:
            @block.sync
            def _(sp):
                sp_setup(sp)
                sp_attention(sp)
                sp_experts(sp)

            @block.gpsimd
            def _(pool):
                pool_setup(pool)
                pool_attention(pool)
                pool_experts(pool)

            @block.scalar
            def _(act):
                act_setup(act)
                act_attention(act)
                act_experts(act)

            @block.vector
            def _(dve):
                dve_setup(dve)
                dve_attention(dve)
                dve_experts(dve)

            @block.tensor
            def _(pe):
                pe_setup(pe)
                pe_attention(pe)
                pe_experts(pe)
        ffn.close()


_INS = ['x', 'ctx_768', 'L0_xattn_Wq', 'L0_xattn_Wk', 'L0_xattn_Wv', 'L0_xattn_Wo', 'L0_xattn_bo', 'L0_ffn_gate_w',
        'L0_ffn_w1', 'L0_ffn_w2']


def kernel(**inputs):
    import numpy as _np
    import concourse.bacc as _bacc
    from concourse import mybir as _mybir
    from concourse.bass_utils import run_bass_kernel_spmd as _run

    nc = _bacc.Bacc("TRN2", target_bir_lowering=False, num_devices=1)
    arrays, args = {}, []
    for name in _INS:
        a = _np.ascontiguousarray(inputs[name])
        arrays[f"in_{name}_dram"] = a
        args.append(nc.dram_tensor(f"in_{name}_dram", a.shape, _mybir.dt.from_np(a.dtype), kind="ExternalInput").ap())
    out = nc.dram_tensor("out_dram", (B, S, D), _mybir.dt.float32, kind="ExternalOutput").ap()
    xattn_expert_choice(nc, *args, out)
    r = _run(nc, [arrays], core_ids=[0])
    return r.results[0]["out_dram"]
```
